# Optimizing a Trainium2 kernel written in Bass

```python
import numpy as np
import jax
import jax.numpy as jnp

def _softmax(x, axis=-1):
    return jax.nn.softmax(x, axis=axis)

def _gelu(x):
    return jax.nn.gelu(x, approximate=True)

def _silu(x):
    return jax.nn.silu(x)

def _sigmoid(x):
    return jax.nn.sigmoid(x)

def _layernorm(x, axis=-1, eps=1e-05):
    m = jnp.mean(x, axis=axis, keepdims=True)
    v = jnp.var(x, axis=axis, keepdims=True)
    return (x - m) / jnp.sqrt(v + eps)

def _scatter_add(tgt, idx, src, axis=0):
    return tgt.at[idx].add(src)

def _segment_sum(src, seg, n):
    return jax.ops.segment_sum(src, seg, n)
kernel_name = 'mk_hybrid_d1_jaxref_r8_58bbe9'

def setup_inputs(seed: int=0):
    np.random.seed(seed)
    _w = jnp.asarray

    def _L0_attn_a_setup():
        import jax, jax.numpy as jnp
        import numpy as np
        D_MODEL = 128
        N_HEADS = 16
        D_HEAD = 64
        BATCH = 4
        SEQ = 256
        NEG = -1000000000.0
        key = jax.random.key(seed)
        k1, k2, k3, k4, k5 = jax.random.split(key, 5)
        x = jax.random.normal(k1, (BATCH, SEQ, D_MODEL), dtype=jnp.float32)
        std = 0.02
        wq = jax.random.normal(k2, (N_HEADS, D_HEAD, D_MODEL), dtype=jnp.float32) * std
        wk = jax.random.normal(k3, (N_HEADS, D_HEAD, D_MODEL), dtype=jnp.float32) * std
        wv = jax.random.normal(k4, (N_HEADS, D_HEAD, D_MODEL), dtype=jnp.float32) * std
        wo = jax.random.normal(k5, (D_MODEL, N_HEADS * D_HEAD), dtype=jnp.float32) * std
        return {'x': x, 'wq': wq, 'wk': wk, 'wv': wv, 'wo': wo}
    _L0_attn_a_in = _L0_attn_a_setup()

    def _L0_attn_b_setup():
        import jax, jax.numpy as jnp
        import numpy as np
        N_HEADS = 16
        key = jax.random.key(seed)
        k_x, k_q, k_k, k_v, k_o = jax.random.split(key, 5)
        N, S, D = (8, 512, 128)
        scale = 0.02
        return {'x': jax.random.normal(k_x, (N, S, D), dtype=jnp.float32), 'Wq': jax.random.normal(k_q, (D, D), dtype=jnp.float32) * scale, 'Wk': jax.random.normal(k_k, (D, D), dtype=jnp.float32) * scale, 'Wv': jax.random.normal(k_v, (D, D), dtype=jnp.float32) * scale, 'Wo': jax.random.normal(k_o, (D, D), dtype=jnp.float32) * scale, 'bo': jnp.zeros((D,), dtype=jnp.float32)}
    _L0_attn_b_in = _L0_attn_b_setup()

    def _L0_ffn_setup():
        import jax, jax.numpy as jnp
        import numpy as np
        B, T, D = (8, 512, 128)
        NUM_SLOTS = 64
        TOP_K = 8
        DQ = D // 4
        DH = D // 2

        def _forward(x, slot_init, w1, b1, w2, b2, tau, Wih, Whh, bih, bhh, wq, bq, wk, bk, wv, bv, ln_g, ln_b, wvp, bvp, wo, bo):
            Bx, Tx, Dx = x.shape
            S = jnp.broadcast_to(slot_init[None], (Bx, NUM_SLOTS, Dx)).astype(x.dtype)
            slot_mean = jnp.broadcast_to(S.mean(axis=1, keepdims=True), (Bx, Tx, Dx))
            ctx = jnp.concatenate([x, slot_mean], axis=-1)
            h = jax.nn.gelu(ctx @ w1 + b1, approximate=False)
            route_logits = (h @ w2 + b2) / (jnp.abs(tau) + 0.1)
            topk_vals, topk_idx = jax.lax.top_k(route_logits, TOP_K)
            topk_w = jax.nn.softmax(topk_vals, axis=-1)
            alpha = (jax.nn.one_hot(topk_idx, NUM_SLOTS, dtype=x.dtype) * topk_w[..., None]).sum(axis=-2)
            slot_input = jnp.einsum('bts,btd->bsd', alpha, x)
            denom = alpha.sum(axis=1) + 1e-08
            si = slot_input / denom[..., None]
            gi = si @ Wih.T + bih
            gh = S @ Whh.T + bhh
            i_r, i_z, i_n = jnp.split(gi, 3, axis=-1)
            h_r, h_z, h_n = jnp.split(gh, 3, axis=-1)
            r = jax.nn.sigmoid(i_r + h_r)
            z = jax.nn.sigmoid(i_z + h_z)
            n = jnp.tanh(i_n + r * h_n)
            S_new = (1.0 - z) * n + z * S
            q = S_new @ wq + bq
            k = S_new @ wk + bk
            v = S_new @ wv + bv
            scale = DQ ** (-0.5)
            attn = jax.nn.softmax(jnp.einsum('bsq,btq->bst', q, k) * scale, axis=-1)
            S_comm = jnp.einsum('bst,btd->bsd', attn, v)
            y = S_new + S_comm
            mu = y.mean(axis=-1, keepdims=True)
            var = y.var(axis=-1, keepdims=True)
            y = (y - mu) * jax.lax.rsqrt(var + 1e-05) * ln_g + ln_b
            slot_values = y @ wvp + bvp
            out = jnp.einsum('bts,bsd->btd', alpha, slot_values)
            return out @ wo + bo
        key = jax.random.key(seed)
        ks = jax.random.split(key, 24)
        n = lambda k, shp, s=0.02: jax.random.normal(k, shp, dtype=jnp.float32) * s
        return {'x': jax.random.normal(ks[0], (B, T, D), dtype=jnp.float32), 'slot_init': n(ks[1], (NUM_SLOTS, D)), 'w1': n(ks[2], (2 * D, DH)), 'b1': jnp.zeros((DH,)), 'w2': n(ks[3], (DH, NUM_SLOTS)), 'b2': jnp.zeros((NUM_SLOTS,)), 'tau': jnp.ones((1,)), 'Wih': n(ks[4], (3 * D, D)), 'Whh': n(ks[5], (3 * D, D)), 'bih': jnp.zeros((3 * D,)), 'bhh': jnp.zeros((3 * D,)), 'wq': n(ks[6], (D, DQ)), 'bq': jnp.zeros((DQ,)), 'wk': n(ks[7], (D, DQ)), 'bk': jnp.zeros((DQ,)), 'wv': n(ks[8], (D, D)), 'bv': jnp.zeros((D,)), 'ln_g': jnp.ones((D,)), 'ln_b': jnp.zeros((D,)), 'wvp': n(ks[9], (D, D)), 'bvp': jnp.zeros((D,)), 'wo': n(ks[10], (D, D)), 'bo': jnp.zeros((D,))}
    _L0_ffn_in = _L0_ffn_setup()
    _d = {'L0_attn_a_x': _L0_attn_a_in['x'], 'L0_attn_a_wq': _L0_attn_a_in['wq'], 'L0_attn_a_wk': _L0_attn_a_in['wk'], 'L0_attn_a_wv': _L0_attn_a_in['wv'], 'L0_attn_a_wo': _L0_attn_a_in['wo'], 'L0_attn_b_Wq': _L0_attn_b_in['Wq'], 'L0_attn_b_Wk': _L0_attn_b_in['Wk'], 'L0_attn_b_Wv': _L0_attn_b_in['Wv'], 'L0_attn_b_Wo': _L0_attn_b_in['Wo'], 'L0_attn_b_bo': _L0_attn_b_in['bo'], 'L0_ffn_slot_init': _L0_ffn_in['slot_init'], 'L0_ffn_w1': _L0_ffn_in['w1'], 'L0_ffn_b1': _L0_ffn_in['b1'], 'L0_ffn_w2': _L0_ffn_in['w2'], 'L0_ffn_b2': _L0_ffn_in['b2'], 'L0_ffn_tau': _L0_ffn_in['tau'], 'L0_ffn_Wih': _L0_ffn_in['Wih'], 'L0_ffn_Whh': _L0_ffn_in['Whh'], 'L0_ffn_bih': _L0_ffn_in['bih'], 'L0_ffn_bhh': _L0_ffn_in['bhh'], 'L0_ffn_wq': _L0_ffn_in['wq'], 'L0_ffn_bq': _L0_ffn_in['bq'], 'L0_ffn_wk': _L0_ffn_in['wk'], 'L0_ffn_bk': _L0_ffn_in['bk'], 'L0_ffn_wv': _L0_ffn_in['wv'], 'L0_ffn_bv': _L0_ffn_in['bv'], 'L0_ffn_ln_g': _L0_ffn_in['ln_g'], 'L0_ffn_ln_b': _L0_ffn_in['ln_b'], 'L0_ffn_wvp': _L0_ffn_in['wvp'], 'L0_ffn_bvp': _L0_ffn_in['bvp'], 'L0_ffn_wo': _L0_ffn_in['wo'], 'L0_ffn_bo': _L0_ffn_in['bo']}
    _x0 = _d['L0_attn_a_x']
    _d['L0_attn_a_x'] = jax.random.normal(jax.random.fold_in(jax.random.key(seed), 1), (16, 256, 128), dtype=_x0.dtype)
    del _x0
    return _d

def reference(L0_attn_a_x, L0_attn_a_wq, L0_attn_a_wk, L0_attn_a_wv, L0_attn_a_wo, L0_attn_b_Wq, L0_attn_b_Wk, L0_attn_b_Wv, L0_attn_b_Wo, L0_attn_b_bo, L0_ffn_slot_init, L0_ffn_w1, L0_ffn_b1, L0_ffn_w2, L0_ffn_b2, L0_ffn_tau, L0_ffn_Wih, L0_ffn_Whh, L0_ffn_bih, L0_ffn_bhh, L0_ffn_wq, L0_ffn_bq, L0_ffn_wk, L0_ffn_bk, L0_ffn_wv, L0_ffn_bv, L0_ffn_ln_g, L0_ffn_ln_b, L0_ffn_wvp, L0_ffn_bvp, L0_ffn_wo, L0_ffn_bo):

    def _L0_attn_a_ref(x, wq, wk, wv, wo):
        import jax, jax.numpy as jnp
        import numpy as np
        D_MODEL = 128
        N_HEADS = 16
        D_HEAD = 64
        BATCH = 4
        SEQ = 256
        NEG = -1000000000.0
        b, s, _ = x.shape
        scale = jnp.sqrt(jnp.asarray(D_HEAD, x.dtype))
        q = jnp.einsum('bsd,hed->bhse', x, wq)
        k = jnp.einsum('bsd,hed->bhse', x, wk)
        v = jnp.einsum('bsd,hed->bhse', x, wv)
        scores = jnp.einsum('bhse,bhte->bhst', q, k) / scale
        causal_mask = jnp.triu(jnp.ones((s, s), dtype=bool), k=1)
        scores = jnp.where(causal_mask, jnp.asarray(NEG, scores.dtype), scores)
        weights = jax.nn.softmax(scores, axis=-1)
        heads = jnp.einsum('bhst,bhte->bhse', weights, v)
        concat = heads.transpose(0, 2, 1, 3).reshape(b, s, N_HEADS * D_HEAD)
        return concat @ wo.T

    def _L0_attn_b_ref(x, Wq, Wk, Wv, Wo, bo):
        import jax, jax.numpy as jnp
        import numpy as np
        N_HEADS = 16
        N, S, D = x.shape
        H = N_HEADS
        hd = D // H
        q = (x @ Wq.T).reshape(N, S, H, hd).transpose(0, 2, 1, 3)
        k = (x @ Wk.T).reshape(N, S, H, hd).transpose(0, 2, 1, 3)
        v = (x @ Wv.T).reshape(N, S, H, hd).transpose(0, 2, 1, 3)
        att = jnp.einsum('nqhd,nkhd->nhqk', q, k)
        att = jax.nn.softmax(att / jnp.sqrt(jnp.asarray(hd, x.dtype)), axis=3)
        out = jnp.einsum('nhqk,nkhd->nqhd', att, v).reshape(N, S, D)
        return out @ Wo.T + bo

    def _L0_ffn_ref(x, slot_init, w1, b1, w2, b2, tau, Wih, Whh, bih, bhh, wq, bq, wk, bk, wv, bv, ln_g, ln_b, wvp, bvp, wo, bo):
        import jax, jax.numpy as jnp
        import numpy as np
        B, T, D = (8, 512, 128)
        NUM_SLOTS = 64
        TOP_K = 8
        DQ = D // 4
        DH = D // 2

        def _forward(x, slot_init, w1, b1, w2, b2, tau, Wih, Whh, bih, bhh, wq, bq, wk, bk, wv, bv, ln_g, ln_b, wvp, bvp, wo, bo):
            Bx, Tx, Dx = x.shape
            S = jnp.broadcast_to(slot_init[None], (Bx, NUM_SLOTS, Dx)).astype(x.dtype)
            slot_mean = jnp.broadcast_to(S.mean(axis=1, keepdims=True), (Bx, Tx, Dx))
            ctx = jnp.concatenate([x, slot_mean], axis=-1)
            h = jax.nn.gelu(ctx @ w1 + b1, approximate=False)
            route_logits = (h @ w2 + b2) / (jnp.abs(tau) + 0.1)
            topk_vals, topk_idx = jax.lax.top_k(route_logits, TOP_K)
            topk_w = jax.nn.softmax(topk_vals, axis=-1)
            alpha = (jax.nn.one_hot(topk_idx, NUM_SLOTS, dtype=x.dtype) * topk_w[..., None]).sum(axis=-2)
            slot_input = jnp.einsum('bts,btd->bsd', alpha, x)
            denom = alpha.sum(axis=1) + 1e-08
            si = slot_input / denom[..., None]
            gi = si @ Wih.T + bih
            gh = S @ Whh.T + bhh
            i_r, i_z, i_n = jnp.split(gi, 3, axis=-1)
            h_r, h_z, h_n = jnp.split(gh, 3, axis=-1)
            r = jax.nn.sigmoid(i_r + h_r)
            z = jax.nn.sigmoid(i_z + h_z)
            n = jnp.tanh(i_n + r * h_n)
            S_new = (1.0 - z) * n + z * S
            q = S_new @ wq + bq
            k = S_new @ wk + bk
            v = S_new @ wv + bv
            scale = DQ ** (-0.5)
            attn = jax.nn.softmax(jnp.einsum('bsq,btq->bst', q, k) * scale, axis=-1)
            S_comm = jnp.einsum('bst,btd->bsd', attn, v)
            y = S_new + S_comm
            mu = y.mean(axis=-1, keepdims=True)
            var = y.var(axis=-1, keepdims=True)
            y = (y - mu) * jax.lax.rsqrt(var + 1e-05) * ln_g + ln_b
            slot_values = y @ wvp + bvp
            out = jnp.einsum('bts,bsd->btd', alpha, slot_values)
            return out @ wo + bo
        return _forward(x, slot_init, w1, b1, w2, b2, tau, Wih, Whh, bih, bhh, wq, bq, wk, bk, wv, bv, ln_g, ln_b, wvp, bvp, wo, bo)
    x = L0_attn_a_x
    x = x + _L0_attn_a_ref(_layernorm(x, axis=-1), L0_attn_a_wq, L0_attn_a_wk, L0_attn_a_wv, L0_attn_a_wo)
    x = x + _L0_ffn_ref(_layernorm(x, axis=-1), L0_ffn_slot_init, L0_ffn_w1, L0_ffn_b1, L0_ffn_w2, L0_ffn_b2, L0_ffn_tau, L0_ffn_Wih, L0_ffn_Whh, L0_ffn_bih, L0_ffn_bhh, L0_ffn_wq, L0_ffn_bq, L0_ffn_wk, L0_ffn_bk, L0_ffn_wv, L0_ffn_bv, L0_ffn_ln_g, L0_ffn_ln_b, L0_ffn_wvp, L0_ffn_bvp, L0_ffn_wo, L0_ffn_bo)
    x = x + _L0_attn_b_ref(_layernorm(x, axis=-1), L0_attn_b_Wq, L0_attn_b_Wk, L0_attn_b_Wv, L0_attn_b_Wo, L0_attn_b_bo)
    x = x + _L0_ffn_ref(_layernorm(x, axis=-1), L0_ffn_slot_init, L0_ffn_w1, L0_ffn_b1, L0_ffn_w2, L0_ffn_b2, L0_ffn_tau, L0_ffn_Wih, L0_ffn_Whh, L0_ffn_bih, L0_ffn_bhh, L0_ffn_wq, L0_ffn_bq, L0_ffn_wk, L0_ffn_bk, L0_ffn_wv, L0_ffn_bv, L0_ffn_ln_g, L0_ffn_ln_b, L0_ffn_wvp, L0_ffn_bvp, L0_ffn_wo, L0_ffn_bo)
    return x

_drawn_inputs = setup_inputs


def setup_inputs(seed=0):
    import zlib

    import numpy as np

    out = dict(_drawn_inputs(seed))
    spreads = {'L0_attn_b_bo': (0.0, 0.1),
     'L0_ffn_b1': (0.0, 0.8),
     'L0_ffn_b2': (0.0, 0.8),
     'L0_ffn_bih': (0.0, 0.1),
     'L0_ffn_bhh': (0.0, 0.354),
     'L0_ffn_bq': (0.0, 2.0),
     'L0_ffn_bk': (0.0, 2.0),
     'L0_ffn_bv': (0.0, 0.1),
     'L0_ffn_ln_g': (1.0, 0.6),
     'L0_ffn_ln_b': (0.0, 0.8),
     'L0_ffn_bvp': (0.0, 0.1),
     'L0_ffn_bo': (0.0, 0.1)}
    factors = {'L0_attn_a_wq': 8.0,
     'L0_attn_a_wk': 8.0,
     'L0_attn_b_Wq': 8.0,
     'L0_attn_b_Wk': 8.0,
     'L0_attn_b_Wv': 4.706,
     'L0_attn_b_Wo': 4.579,
     'L0_ffn_slot_init': 8.0,
     'L0_ffn_w1': 8.0,
     'L0_ffn_w2': 8.0,
     'L0_ffn_Wih': 5.427,
     'L0_ffn_Whh': 8.0,
     'L0_ffn_wq': 64.0,
     'L0_ffn_wk': 34.231,
     'L0_ffn_wv': 5.589}
    for name, (base, spread) in spreads.items():
        noise = np.random.default_rng([zlib.crc32(name.encode()), seed]).standard_normal(out[name].shape)
        drawn = base * np.exp(spread * noise) if base else spread * noise
        out[name] = jnp.asarray(drawn.astype(out[name].dtype))
    for name, factor in factors.items():
        out[name] = (out[name] * factor).astype(out[name].dtype)
    return out
```

```python
import concourse.bass as bass
from concourse import mybir
from contextlib import ExitStack
import numpy as np

F32 = mybir.dt.float32
F16 = mybir.dt.float16
BF16 = mybir.dt.bfloat16
ACT = mybir.ActivationFunctionType
ALU = mybir.AluOpType
X_AXIS = mybir.AxisListType.X

NB, SEQ, D = 16, 256, 128
NT = NB * SEQ // 128
QT = SEQ // 128
H = 16
EA = 64
EB = D // H
GA = H // 4
NS, TOPK, DQ, DH = 64, 8, D // 4, D // 2
EPS = 1e-5
V_UP = 32.0
CHUNKS = 2
CB = NB // CHUNKS
CT = CB * QT
PAIRS = CB // 2
MASKED = -1e30
TAKEN = -3e38
W = EA + 1
ROLLS = H // 2
HV = 10
TB = 8


class Chain:

    def __init__(self, eng, sem):
        self.eng, self.sem, self.count, self.looped = eng, sem, 0, 0

    def link(self, ins):
        self.count += 1
        ins.then_inc(self.sem, 1)
        self.eng.wait_ge(self.sem, self.looped + self.count)

    def enter(self, trip, per):
        self.looped, self.before, self.per = trip * per, self.count, per

    def leave(self, trips):
        assert self.count - self.before == self.per, (self.count - self.before, self.per)
        self.looped, self.count = 0, self.before + trips * self.per




def a_steps(first=False, last=False):
    steps = []
    for g in range(GA):
        prepare = not (last and g == GA - 1)

        def put(cond, *new):
            steps.extend((kind, g, n) for kind, n in new if cond)
        put(True, ("exps", 0))
        put(prepare, ("qk", 0))
        put(True, ("exps", 1))
        put(prepare, ("qk", 1))
        put(True, ("exps", 2))
        put(g == 1 and not first, ("project", 0))
        put(prepare, ("max", 0), ("v", 0), ("max", 1))
        put(True, ("pv", 0))
        put(prepare, ("max", 2))
        put(True, ("pv", 1))
        put(not (first and g == 0), ("turn", 0))
        put(g == 1 and not last, ("norm", 0))
        put(g == 2 and not last, ("apply", 0), ("xt", 0))
        put(prepare, ("maxrow", 0))
        put(True, ("normal", 0))
    return steps


def b_steps(par, first=False, ahead=True, ahead2=True):
    one, two = ahead, ahead2
    steps = []

    def put(cond, *names):
        if cond:
            steps.extend((n[0], par, n[1]) if isinstance(n, tuple) else (n, par, 0) for n in names)
    put(one, "qk")
    put(True, "soft")
    put(one, "v", ("roll", 0), ("roll", 1))
    put(not first, ("gather", 1), "expand")
    put(True, "sumexp", ("weigh", 0))
    put(one, ("dot", 0), ("roll", 2), ("dot", 1), ("roll", 3), ("dot", 2))
    put(not first, "project")
    put(one, ("roll", 4), ("dot", 3))
    put(True, ("weigh", 1))
    put(one, ("roll", 5), ("dot", 4))
    put(two, "norm")
    put(one, ("roll", 6), ("dot", 5))
    put(two, "apply", "xt")
    put(one, ("roll", 7))
    put(True, ("gather", 0))
    put(one, ("dot", 6), ("dot", 7))
    return steps


A_PROLOGUE = [("norm", 3, 0), ("apply", 3, 0), ("xt", 3, 0), ("qk", 3, 0), ("qk", 3, 1), ("v", 3, 0),
              ("max", 3, 0), ("max", 3, 1), ("max", 3, 2), ("maxrow", 3, 0)]
A_EPILOGUE = [("turn", 0, 0), ("project", 0, 0)]
B_PROLOGUE = [("norm", 0, 0), ("apply", 0, 0), ("xt", 0, 0), ("qk", 1, 0), ("v", 1, 0), ("roll", 1, 0)]
for m in range(1, ROLLS):
    B_PROLOGUE += [("roll", 1, m), ("dot", 1, m - 1)]
B_PROLOGUE += [("dot", 1, ROLLS - 1), ("norm", 1, 0), ("apply", 1, 0), ("xt", 1, 0)]
B_EPILOGUE = [("gather", 0, 1), ("expand", 0, 0), ("project", 0, 0)]

R_STEPS = ("qk", "v", "turn", "project", "xt", "maxrow")


def fills_of(steps):
    return [s for s in steps if s[0] in R_STEPS]


A_PLAN = [(A_PROLOGUE, -1, None), (a_steps(first=True), 0, None), (a_steps(), 1, NB - 2),
          (a_steps(last=True), NB - 1, None), (A_EPILOGUE, NB, None)]
B_PLAN = [(B_PROLOGUE, -1, None), (b_steps(0, first=True) + b_steps(1), 0, None),
          (b_steps(0) + b_steps(1), 1, NB // 2 - 2),
          (b_steps(0, ahead2=False) + b_steps(1, ahead=False, ahead2=False), NB // 2 - 1, None),
          (B_EPILOGUE, NB // 2, None)]


class Fill:

    def __init__(self, number, looped, former):
        self.bank, self.count, self.former = number % 2, number + 1 + looped, former


def run_plan(eng, plan, do, chain=None, per=0):
    number, history = 0, []
    for steps, index, trips in plan:
        mine = fills_of(steps)
        if trips:
            assert len(mine) % 2 == 0 and [f[0] for f in history[-2:]] == mine[-2:]
            with eng.Fori(0, trips) as i:
                if chain:
                    chain.enter(i, per)
                past, k = [(f, index - 1 + i) for f in mine[-2:]], 0
                for step in steps:
                    fill = None
                    if step[0] in R_STEPS:
                        fill = Fill(number + k, i * len(mine), past[-2])
                        past.append((step, index + i))
                        k += 1
                    do(step, index + i, fill)
            if chain:
                chain.leave(trips)
            history += [(f, index + trips - 1) for f in mine]
            number += trips * len(mine)
        else:
            for step in steps:
                fill = None
                if step[0] in R_STEPS:
                    fill = Fill(number, 0, history[-2] if len(history) >= 2 else None)
                    history.append((step, index))
                    number += 1
                do(step, index, fill)


WEIGHTS = ["ident", "identb", "mask_q", "mask_k", "onehot", "roll", "heads", "rowmask",
           "a_wqk", "a_wv", "a_wo", "b_wqkv", "b_wo", "b_bo", "slot", "slot_t", "w1a", "w1b", "b1", "w2b", "tau",
           "wih_t", "whh_t", "bih", "bhh", "wq", "bq", "wk", "bk", "wv", "bv", "ln_g", "ln_b", "wvp", "wvp_t",
           "bvp", "wo", "bo"]


def build(nc, x_in, w_in, out):
    ctx = ExitStack()
    with ctx:
        def sb(name, shape, dt=F32, stage=ctx):
            return stage.enter_context(nc.sbuf_tensor(name, shape, dt))

        def sem(name):
            return ctx.enter_context(nc.semaphore(name))

        w = {n: sb("w_" + n, list(w_in[n].shape), w_in[n].dtype) for n in WEIGHTS}
        ident, identb = w["ident"], w["identb"]
        ones = sb("ones", [128, 128])
        a_wqk_h, a_wqk_l = sb("a_wqk_h", [128, 8, 2, 128], F16), sb("a_wqk_l", [128, 8, 2, 128], F16)
        a_wv_h, a_wv_l = sb("a_wv_h", [128, H * EA], F16), sb("a_wv_l", [128, H * EA], F16)
        b_w_h, b_w_l = sb("b_w_h", [128, 3, 128], F16), sb("b_w_l", [128, 3, 128], F16)
        w2s = sb("w2s", [NS + 1, NS])
        inv_tau = sb("inv_tau", [NS + 1, 2])
        slot_mean, c1 = sb("slot_mean", [128, 1]), sb("c1", [DH, 1])
        brz, bn_half = sb("brz", [128, 2]), sb("bn_half", [128, 1])
        gate_h, hn_half = sb("gate_h", [128, 2, NS]), sb("hn_half", [128, NS])
        cmid, wcomb, crow = sb("cmid", [128, 1]), sb("wcomb", [128, 128]), sb("crow", [1, 128])
        minus_half, eps = sb("minus_half", [128, CT]), sb("eps", [128, CT])

        X = sb("X", [128, NT, D])
        stats, mv = sb("stats", [128, CT, 6]), sb("mv", [128, CT, 2])
        veps, rstd = sb("veps", [128, CT]), sb("rstd", [128, CT])
        xn = sb("xn", [128, QT, D])
        gate = sb("gate", [128, 1])
        xh, xl = sb("xh", [128, SEQ], F16), sb("xl", [128, SEQ], F16)

        a_v = sb("a_v", [128, 2, QT, 4, W])

        f_xs = sb("f_xs", [128, CT, D + 1])
        f_xt = sb("f_xt", [128, CT * 128])
        f_h = sb("f_h", [DH + 1, CT * 128])
        f_v8 = sb("f_v8", [128, CT, TOPK])
        f_z, f_e = sb("f_z", [128, CT, NS]), sb("f_e", [128, CT, NS])
        f_sum = sb("f_sum", [128, CT])
        f_al = sb("f_al", [128, CT, NS])
        f_alt = sb("f_alt", [128, CT // 2, 128])
        f_den = sb("f_den", [128, PAIRS])
        f_si, f_sit = sb("f_si", [128, PAIRS, D]), sb("f_sit", [128, 512])
        f_r, f_zg, f_n, f_t = (sb(n, [128, 512]) for n in ("f_r", "f_zg", "f_n", "f_t"))
        f_sn = sb("f_sn", [128, 512])
        f_q, f_k, f_v = sb("f_q", [DQ, 512]), sb("f_k", [DQ, 512]), sb("f_v", [128, PAIRS, D])
        f_m, f_rs = sb("f_m", [128, PAIRS]), sb("f_rs", [128, PAIRS])
        f_s = sb("f_s", [128, PAIRS, NS])
        f_p = sb("f_p", [128, PAIRS, 2 * NS])
        f_pt = sb("f_pt", [128, 512])
        f_y, f_yt = sb("f_y", [128, PAIRS, D]), sb("f_yt", [128, 512])
        f_so = sb("f_so", [128, PAIRS, D])

        with ExitStack() as in_a:
            a_qk_h = sb("a_qk_h", [128, 2, 2, 2, SEQ], F16, stage=in_a)
            a_qk_l = sb("a_qk_l", [128, 2, 2, 2, SEQ], F16, stage=in_a)
            a_nm, a_nmt = sb("a_nm", [128, 2, QT, 4], BF16, stage=in_a), sb("a_nmt", [4, 2, SEQ], BF16, stage=in_a)
            a_p = sb("a_p", [128, 2, 3, 512], stage=in_a)
            a_rs = sb("a_rs", [128, QT, 4], stage=in_a)
            a_o = sb("a_o", [128, 2, QT, 4, EA], stage=in_a)
            a_ot = sb("a_ot", [128, 8, SEQ], stage=in_a)

        b_qt = sb("b_qt", [128, SEQ])
        b_kh, b_kl = sb("b_kh", [128, SEQ], F16), sb("b_kl", [128, SEQ], F16)
        b_prod = sb("b_prod", [128, 2, 2, SEQ])
        b_v = sb("b_v", [128, 2, QT, 2 * H, EB])
        b_e = sb("b_e", [128, 2, QT, H, H])
        b_m, b_rs = sb("b_m", [128, QT, H]), sb("b_rs", [128, 2, QT, H])
        b_w8 = sb("b_w8", [128, QT, H, EB, H])
        b_s = sb("b_s", [128, 2, QT, H * EB])
        b_o = sb("b_o", [128, QT, H, EB])
        b_ox = sb("b_ox", [128, QT, EB, H, TB])

        PS = [ctx.enter_context(nc.psum_tensor(f"PS{i}", [128, 512], F32)) for i in range(8)]
        R, T, M, O = PS[0:2], PS[2:4], PS[4:6], PS[6:8]
        RB16 = [r[:, :].bitcast(BF16) for r in R]

        x_loaded, w_loaded, stored = sem("x_loaded"), sem("w_loaded"), sem("stored")
        dve_chain, pool_chain = sem("dve_chain"), sem("pool_chain")
        pool_set, dve_set = sem("pool_set"), sem("dve_set")
        set_mm, set_ev = sem("set_mm"), sem("set_ev")

        def mm3(pe, dst, ah, al, bh, bl, start, stop):
            pe.matmul(dst, ah, bh, start=start, stop=False, skip_group_check=True)
            pe.matmul(dst, ah, bl, start=False, stop=False, skip_group_check=True)
            return pe.matmul(dst, al, bh, start=False, stop=stop, skip_group_check=True)

        def wait(eng, semaphore, value):
            if not (isinstance(value, int) and value <= 0):
                eng.wait_ge(semaphore, value)

        def norm_stats(dve, link, X, tile, n):
            for t in range(n):
                ins = dve.bn_stats(stats[:, t, :], X[:, bass.ds(tile + t, 1), :].rearrange("p a d -> p (a d)"))
            link(ins)
            dve.memset(gate[:, :], 0.0)
            for t in range(n):
                ins = dve.bn_aggr(mv[:, t, :], stats[:, t, :])
            return ins

        def norm_rstd(pool, link, n):
            link(pool.tensor_tensor(veps[:, 0:n], mv[:, 0:n, 1], eps[:, 0:n], ALU.add))
            return pool.tensor_tensor(rstd[:, 0:n], veps[:, 0:n], minus_half[:, 0:n], ALU.pow)

        def norm_apply(dve, X, tile, n, dst):
            for t in range(n):
                ins = dve.tensor_scalar(dst[:, t, 0:D], X[:, bass.ds(tile + t, 1), :].rearrange("p a d -> p (a d)"),
                                        mv[:, t, 0:1], rstd[:, t:t + 1], ALU.subtract, ALU.mult)
            return ins

        a_filled = sem("a_filled")
        a_stats, a_rstd, a_normed = sem("a_stats"), sem("a_rstd"), sem("a_normed")
        a_xh, a_xl = sem("a_xh"), sem("a_xl")
        a_hi, a_lo, a_values, a_maxrow = sem("a_hi"), sem("a_lo"), sem("a_values"), sem("a_maxrow")
        a_max_mm, a_maxed = sem("a_max_mm"), sem("a_maxed")
        a_exp_mm, a_exped = sem("a_exp_mm"), sem("a_exped")
        a_pv, a_normal, a_turned, a_added = sem("a_pv"), sem("a_normal"), sem("a_turned"), sem("a_added")

        def a_read(step, b):
            kind, g, j = step
            u = GA * b + g
            return {"qk": (a_lo, 2 * (u + 1) + j + 1), "v": (a_values, u + 2), "maxrow": (a_maxrow, u + 2),
                    "turn": (a_turned, u), "project": (a_added, b), "xt": (a_xl, b + 2)}[kind]

        def bank3(g, j):
            return (3 * g + j) % 2

        a_even = sem("a_even")

        def evens(u, exps):
            return 2 * u + exps + 1

        def a_tensor(pe):
            def do(step, b, fill):
                kind, g, j = step
                u = GA * b + g
                me, nx = g % 2, (g + 1) % 2
                if fill:
                    dst = R[fill.bank]
                    if fill.former:
                        wait(pe, *a_read(*fill.former))
                if kind == "xt":
                    pe.wait_ge(a_normed, b + 2)
                    for t in range(QT):
                        ins = pe.transpose(dst[:, t * 128:(t + 1) * 128], xn[:, t, :], ident[:, :])
                    ins.then_inc(a_filled, 1)
                elif kind == "qk":
                    pair = 2 * ((g + 1) % GA) + j
                    if g == GA - 1 and j == 0:
                        pe.wait_ge(a_xl, b + 2)
                    for z in range(2):
                        ins = mm3(pe, dst[:, z * SEQ:(z + 1) * SEQ], a_wqk_h[:, pair, z, :], a_wqk_l[:, pair, z, :],
                                  xh[:, :], xl[:, :], z == 0, z == 1)
                    ins.then_inc(a_filled, 1)
                elif kind == "v":
                    c = ((g + 1) % GA) * 4 * EA
                    for t in range(QT):
                        tok = slice(t * 128, t * 128 + 128)
                        ins = mm3(pe, dst[:, t * 256:(t + 1) * 256], xh[:, tok], xl[:, tok],
                                  a_wv_h[:, c:c + 256], a_wv_l[:, c:c + 256], t == 0, t == 1)
                    ins.then_inc(a_filled, 1)
                elif kind == "max":
                    m = 3 * (u + 1) + j
                    wait(pe, a_maxed, m - 1)
                    if j == 0:
                        pe.wait_ge(a_hi, 2 * (u + 1) + 2)
                    dst = M[bank3(g + 1, j)]
                    if j == 0:
                        for i, h in enumerate((0, 2, 1, 3)):
                            p = slice(64 * (h % 2), 64 * (h % 2) + 64)
                            if i == 2:
                                ins.then_inc(a_even, 1)
                                pe.matmul(dst[:, :], identb[:, :], w["mask_q"][:, :, :], start=False, stop=False,
                                          skip_group_check=True)
                                pe.wait_ge(a_even, evens(u + 1, 0))
                            ins = pe.matmul(dst[:, h * 128:(h + 1) * 128], a_qk_h[p, nx, h // 2, 0, 0:128],
                                            a_qk_h[p, nx, h // 2, 1, 0:128], start=i == 0, stop=i == 3,
                                            skip_group_check=True)
                    else:
                        p = slice(64 * (j - 1), 64 * (j - 1) + 64)
                        for pair in range(2):
                            pe.matmul(dst[:, pair * 256:(pair + 1) * 256], a_qk_h[p, nx, pair, 0, 128:256],
                                      a_qk_h[p, nx, pair, 1, :], start=pair == 0, stop=False, skip_group_check=True)
                        ins = pe.matmul(dst[:, :].rearrange("p (h k) -> p h k", h=2)[:, :, 128:256], identb[:, :],
                                        w["mask_q"][:, 0:2, :], start=False, stop=True, skip_group_check=True)
                    ins.then_inc(a_max_mm, 1)
                elif kind == "maxrow":
                    pe.wait_ge(a_maxed, 3 * (u + 1) + 3)
                    for t in range(QT):
                        ins = pe.transpose(RB16[fill.bank][0:4, t * 128:(t + 1) * 128], a_nm[:, nx, t, :],
                                           identb[:, :])
                    ins.then_inc(a_filled, 1)
                elif kind == "exps":
                    n = 3 * u + j
                    wait(pe, a_exped, n - 1)
                    if j == 0:
                        pe.wait_ge(a_lo, 2 * u + 2)
                    dst = T[bank3(g, j)]
                    heads, wd, q0, k0 = ((j, j + 2), 256, 0, 0) if j < 2 else ((0, 2, 1, 3), 128, 128, 128)
                    for i, h in enumerate(heads):
                        p, keys, qs = slice(64 * (h % 2), 64 * (h % 2) + 64), slice(k0, k0 + 128), slice(q0, 256)
                        if i == 2:
                            ins.then_inc(a_even, 1)
                            pe.matmul(dst[:, :], identb[:, :], w["mask_k"][:, :, :], start=False, stop=False,
                                      skip_group_check=True)
                            pe.wait_ge(a_even, evens(u, 1))
                        ins = mm3(pe, dst[:, i * wd:(i + 1) * wd],
                            a_qk_h[p, me, h // 2, 1, keys], a_qk_l[p, me, h // 2, 1, keys],
                            a_qk_h[p, me, h // 2, 0, qs], a_qk_l[p, me, h // 2, 0, qs], i == 0, False)
                    if j < 2:
                        pe.matmul(dst[:, :].rearrange("p (h q) -> p h q", h=2)[:, :, 0:128], identb[:, :],
                                  w["mask_k"][:, 0:2, :], start=False, stop=False, skip_group_check=True)
                    if j == 0:
                        pe.wait_ge(a_maxrow, u + 1)
                    for i, h in enumerate(heads):
                        ins = pe.matmul(dst[:, i * wd:(i + 1) * wd], w["onehot"][:, h, :], a_nmt[:, me, q0:256],
                                        start=False, stop=i == len(heads) - 1, skip_group_check=True)
                    ins.then_inc(a_exp_mm, 1)
                elif kind == "pv":
                    q = j
                    if q == 0:
                        pe.wait_ge(a_values, u + 1)
                        wait(pe, a_normal, u)
                    pe.wait_ge(a_exped, 3 * u + 2 + q)
                    for h in range(4):
                        for k in range(q + 1):
                            c = (h // 2) * 256 + q * 128 if k == 0 else (0, 2, 1, 3)[h] * 128
                            ins = pe.matmul(O[q][:, h * W:(h + 1) * W],
                                            a_p[:, me, h % 2 if k == 0 else 2, c:c + 128], a_v[:, me, k, h, :],
                                            start=h == 0 and k == 0, stop=h == 3 and k == q, skip_group_check=True)
                    ins.then_inc(a_pv, 1)
                elif kind == "turn":
                    pe.wait_ge(a_normal, u)
                    for pair in range(2):
                        for t in range(QT):
                            c = (2 * pair + t) * 128
                            ins = pe.transpose(dst[:, c:c + 128], a_o[:, nx, t, 2 * pair:2 * pair + 2, :]
                                               .rearrange("p h e -> p (h e)"), ident[:, :])
                    ins.then_inc(a_filled, 1)
                elif kind == "project":
                    pe.wait_ge(a_turned, GA * b)
                    for t in range(QT):
                        for c in range(8):
                            ins = pe.matmul(dst[:, t * 128:(t + 1) * 128], a_ot[:, c, t * 128:(t + 1) * 128],
                                            w["a_wo"][:, c, :], start=c == 0, stop=c == 7)
                    ins.then_inc(a_filled, 1)
            run_plan(pe, A_PLAN, do)

        def a_scalar(act):
            def do(step, b, fill):
                kind, g, j = step
                u = GA * b + g
                me, nx = g % 2, (g + 1) % 2
                if kind in ("xt", "qk", "v", "turn"):
                    act.wait_ge(a_filled, fill.count)
                    src = R[fill.bank]
                if kind == "xt":
                    act.activation(xh[:, :], src[:, 0:SEQ], ACT.Copy).then_inc(a_xh, 1)
                elif kind == "qk":
                    act.activation(a_qk_h[:, nx, j, :, :].rearrange("p z t -> p (z t)"), src[:, :],
                                   ACT.Copy).then_inc(a_hi, 1)
                elif kind == "v":
                    act.activation(a_v[:, nx, :, :, 0:EA], src[:, :].rearrange("p (t h e) -> p t h e", t=QT, h=4),
                                   ACT.Copy, scale=1.0 / V_UP).then_inc(a_values, 1)
                elif kind == "exps":
                    act.wait_ge(a_exp_mm, 3 * u + j + 1)
                    act.activation(a_p[:, me, j, :], T[bank3(g, j)][:, :], ACT.Exp,
                                   scale=EA ** -0.5).then_inc(a_exped, 1)
                elif kind == "turn":
                    c = 2 * ((g - 1) % GA)
                    act.activation(a_ot[:, c:c + 2, :], src[:, :].rearrange("p (c t) -> p c t", c=2),
                                   ACT.Copy).then_inc(a_turned, 1)
            run_plan(act, A_PLAN, do)

        def a_vector(dve, chain):
            link = chain.link

            def do(step, b, fill):
                kind, g, j = step
                u = GA * b + g
                me, nx = g % 2, (g + 1) % 2
                if kind == "norm":
                    norm_stats(dve, link, X, (b + 1) * QT, QT).then_inc(a_stats, 1)
                elif kind == "apply":
                    dve.wait_ge(a_rstd, b + 2)
                    norm_apply(dve, X, (b + 1) * QT, QT, xn).then_inc(a_normed, 1)
                elif kind == "xt":
                    dve.wait_ge(a_xh, b + 2)
                    dve.tensor_tensor(xl[:, :], R[fill.bank][:, 0:SEQ], xh[:, :], ALU.subtract).then_inc(a_xl, 1)
                elif kind == "qk":
                    dve.wait_ge(a_hi, 2 * (u + 1) + j + 1)
                    dve.tensor_tensor(a_qk_l[:, nx, j, :, :].rearrange("p z t -> p (z t)"), R[fill.bank][:, :],
                                      a_qk_h[:, nx, j, :, :].rearrange("p z t -> p (z t)"),
                                      ALU.subtract).then_inc(a_lo, 1)
                elif kind == "max":
                    dve.wait_ge(a_max_mm, 3 * (u + 1) + j + 1)
                    dst = a_nm[:, nx, 0, :] if j == 0 else a_nm[:, nx, 1, j - 1:4:2]
                    dve.tensor_reduce(dst, M[bank3(g + 1, j)][:, :].rearrange("p (h k) -> p h k", h=4 if j == 0 else 2),
                                      X_AXIS, ALU.max, negate=True).then_inc(a_maxed, 1)
                elif kind == "maxrow":
                    dve.wait_ge(a_filled, fill.count)
                    dve.tensor_copy(a_nmt[:, nx, :], RB16[fill.bank][0:4, 0:SEQ]).then_inc(a_maxrow, 1)
                elif kind == "normal":
                    dve.wait_ge(a_pv, 2 * u + 2)
                    for q in range(QT):
                        o = O[q][:, 0:4 * W].rearrange("p (h e) -> p h e", h=4)
                        ins = dve.reciprocal(a_rs[:, q, :], o[:, :, EA:EA + 1].rearrange("p h a -> p (h a)"))
                    link(ins)
                    for q in range(QT):
                        o = O[q][:, 0:4 * W].rearrange("p (h e) -> p h e", h=4)
                        ins = dve.tensor_tensor(a_o[:, me, q, :, :], o[:, :, 0:EA],
                                                a_rs[:, q, :].unsqueeze(2).to_broadcast([128, 4, EA]), ALU.mult)
                    ins.then_inc(a_normal, 1)
                elif kind == "project":
                    dve.wait_ge(a_filled, fill.count)
                    xb = X[:, bass.ds((b - 1) * QT, QT), :]
                    dve.tensor_tensor(xb, R[fill.bank][:, 0:SEQ].rearrange("p (t d) -> p t d", t=QT), xb,
                                      ALU.add).then_inc(a_added, 1)
            run_plan(dve, A_PLAN, do, chain, 1 + GA)
            dve.wait_ge(a_added, NB)

        def a_gpsimd(pool, chain):
            def do(step, b, fill):
                if step[0] == "norm":
                    pool.wait_ge(a_stats, b + 2)
                    norm_rstd(pool, chain.link, QT).then_inc(a_rstd, 1)
            run_plan(pool, A_PLAN, do, chain, 1)

        b_filled = sem("b_filled")
        b_stats, b_rstd, b_normed = sem("b_stats"), sem("b_rstd"), sem("b_normed")
        b_xh, b_xl, b_hi, b_lo, b_values = sem("b_xh"), sem("b_xl"), sem("b_hi"), sem("b_lo"), sem("b_values")
        b_rolled, b_multiplied, b_dotted = sem("b_rolled"), sem("b_multiplied"), sem("b_dotted")
        b_shifted, b_exped, b_weighed, b_normal = sem("b_shifted"), sem("b_exped"), sem("b_weighed"), sem("b_normal")
        b_gathered, b_expanded, b_added = sem("b_gathered"), sem("b_expanded"), sem("b_added")

        def rolled_values(par, t, h0, n):
            v = b_v[:, par, t, h0:h0 + 1, 0:1]
            return bass.AP(v.tensor, v.offset, [list(v.ap[0]), [EB, n], [1, EB], [EB, H]])

        def rolled_exps(par, t, h0, n):
            x = b_e[:, par, t, 0:1, h0:h0 + 1]
            return bass.AP(x.tensor, x.offset, [list(x.ap[0]), [1, n], [0, EB], [H, H]])

        def b_read(step, i):
            kind, par, j = step
            b = 2 * i + par
            return {"qk": (b_lo, b + 2), "v": (b_values, b + 2), "project": (b_added, b), "xt": (b_xl, b + 3)}[kind]

        def b_tensor(pe):
            def do(step, i, fill):
                kind, par, j = step
                b = 2 * i + par
                nx = 1 - par
                if fill:
                    dst = R[fill.bank]
                    if fill.former:
                        wait(pe, *b_read(*fill.former))
                if kind == "xt":
                    pe.wait_ge(b_normed, b + 3)
                    for t in range(QT):
                        ins = pe.transpose(dst[:, t * 128:(t + 1) * 128], xn[:, t, :], ident[:, :])
                    ins.then_inc(b_filled, 1)
                elif kind == "qk":
                    pe.wait_ge(b_xl, b + 2)
                    for z in range(2):
                        ins = mm3(pe, dst[:, z * SEQ:(z + 1) * SEQ], b_w_h[:, z, :], b_w_l[:, z, :],
                                  xh[:, :], xl[:, :], z == 0, z == 1)
                    ins.then_inc(b_filled, 1)
                elif kind == "v":
                    for t in range(QT):
                        tok = slice(t * 128, t * 128 + 128)
                        ins = mm3(pe, dst[:, t * 128:(t + 1) * 128], xh[:, tok], xl[:, tok],
                                  b_w_h[:, 2, :], b_w_l[:, 2, :], t == 0, t == 1)
                    ins.then_inc(b_filled, 1)
                elif kind == "roll":
                    m = ROLLS * (b + 1) + j
                    if j == 0:
                        pe.wait_ge(b_lo, b + 2)
                    wait(pe, b_multiplied, m - 1)
                    for e in range(2):
                        pe.matmul(T[j % 2][:, e * SEQ:(e + 1) * SEQ], w["roll"][:, 2 * j + e, :], b_kh[:, :],
                                  start=e == 0, stop=False, skip_group_check=True)
                        ins = pe.matmul(T[j % 2][:, e * SEQ:(e + 1) * SEQ], w["roll"][:, 2 * j + e, :], b_kl[:, :],
                                        start=False, stop=e == 1, skip_group_check=True)
                    ins.then_inc(b_rolled, 1)
                elif kind == "dot":
                    if j == 0:
                        wait(pe, b_shifted, b)
                    pe.wait_ge(b_multiplied, ROLLS * (b + 1) + j + 1)
                    for e in range(2):
                        for t in range(QT):
                            c = (t * H + 2 * j + e) * H
                            ins = pe.matmul(O[nx][:, c:c + H], b_prod[:, j % 2, e, t * 128:(t + 1) * 128],
                                            w["heads"][:, :], start=True, stop=True)
                    ins.then_inc(b_dotted, 1)
                elif kind == "project":
                    pe.wait_ge(b_expanded, b)
                    for t in range(QT):
                        for e in range(EB):
                            pe.matmul(dst[:, t * 128:(t + 1) * 128], b_ox[:, t, e, :, :].rearrange("p h r -> p (h r)"),
                                      w["b_wo"][:, e, :], start=e == 0, stop=False)
                        ins = pe.matmul(dst[:, t * 128:(t + 1) * 128], ones[0:1, :], w["b_bo"][:, :],
                                        start=False, stop=True)
                    ins.then_inc(b_filled, 1)
            run_plan(pe, B_PLAN, do)

        def b_scalar(act):
            def do(step, i, fill):
                kind, par, j = step
                b = 2 * i + par
                if kind in ("xt", "qk", "v"):
                    act.wait_ge(b_filled, fill.count)
                    src = R[fill.bank]
                if kind == "xt":
                    act.activation(xh[:, :], src[:, 0:SEQ], ACT.Copy).then_inc(b_xh, 1)
                elif kind == "qk":
                    act.activation(b_qt[:, :], src[:, 0:SEQ], ACT.Copy)
                    act.activation(b_kh[:, :], src[:, SEQ:2 * SEQ], ACT.Copy).then_inc(b_hi, 1)
                elif kind == "v":
                    wait(act, b_weighed, QT * b)
                    for n in range(2):
                        ins = act.activation(b_v[:, 1 - par, :, n * H:(n + 1) * H, :].rearrange("p t h e -> p t (h e)"),
                                             src[:, 0:SEQ].rearrange("p (t c) -> p t c", t=QT), ACT.Copy)
                    ins.then_inc(b_values, 1)
                elif kind == "soft":
                    act.wait_ge(b_shifted, b + 1)
                    act.activation(b_e[:, par, :, :, :], b_e[:, par, :, :, :], ACT.Exp, scale=EB ** -0.5).then_inc(b_exped, 1)
                elif kind == "expand":
                    act.wait_ge(b_normal, b)
                    for r in range(TB):
                        for t in range(QT):
                            ins = act.activation(b_ox[:, t, :, :, r], b_o[:, t, :, :].rearrange("p h e -> p e h"),
                                                 ACT.Copy, scale=w["rowmask"][:, r:r + 1])
                    ins.then_inc(b_expanded, 1)
            run_plan(act, B_PLAN, do)

        def b_vector(dve, chain):
            link = chain.link

            def do(step, i, fill):
                kind, par, j = step
                b = 2 * i + par
                if kind == "norm":
                    norm_stats(dve, link, X, (b + 2) * QT, QT).then_inc(b_stats, 1)
                elif kind == "apply":
                    dve.wait_ge(b_rstd, b + 3)
                    norm_apply(dve, X, (b + 2) * QT, QT, xn).then_inc(b_normed, 1)
                elif kind == "xt":
                    dve.wait_ge(b_xh, b + 3)
                    dve.tensor_tensor(xl[:, :], R[fill.bank][:, 0:SEQ], xh[:, :], ALU.subtract).then_inc(b_xl, 1)
                elif kind == "qk":
                    dve.wait_ge(b_hi, b + 2)
                    dve.tensor_tensor(b_kl[:, :], R[fill.bank][:, SEQ:2 * SEQ], b_kh[:, :],
                                      ALU.subtract).then_inc(b_lo, 1)
                elif kind == "roll":
                    dve.wait_ge(b_rolled, ROLLS * (b + 1) + j + 1)
                    dve.tensor_tensor(b_prod[:, j % 2, :, :], T[j % 2][:, :].rearrange("p (e t) -> p e t", e=2),
                                      b_qt[:, :].unsqueeze(1).to_broadcast([128, 2, SEQ]),
                                      ALU.mult).then_inc(b_multiplied, 1)
                elif kind == "soft":
                    dve.wait_ge(b_dotted, ROLLS * (b + 1))
                    sc = O[par][:, :].rearrange("p (t s h) -> p t s h", t=QT, s=H)
                    for t in range(QT):
                        ins = dve.tensor_reduce(b_m[:, t, :], sc[:, t, :, :].rearrange("p s h -> p h s"), X_AXIS, ALU.max)
                    link(ins)
                    for t in range(QT):
                        ins = dve.tensor_tensor(b_e[:, par, t, :, :], sc[:, t, :, :],
                                                b_m[:, t, :].unsqueeze(1).to_broadcast([128, H, H]), ALU.subtract)
                    ins.then_inc(b_shifted, 1)
                elif kind == "sumexp":
                    dve.wait_ge(b_exped, b + 1)
                    for t in range(QT):
                        ins = dve.tensor_reduce(b_rs[:, par, t, :], b_e[:, par, t, :, :].rearrange("p s h -> p h s"),
                                                X_AXIS, ALU.add)
                    link(ins)
                    link(dve.reciprocal(b_rs[:, par, :, :].rearrange("p t h -> p (t h)"),
                                        b_rs[:, par, :, :].rearrange("p t h -> p (t h)")))
                elif kind == "weigh" and j == 0:
                    dve.wait_ge(b_values, b + 1)
                    link(dve.tensor_tensor(b_w8[:, 0, 0:HV, :, :], rolled_values(par, 0, 0, HV),
                                           rolled_exps(par, 0, 0, HV), ALU.mult))
                elif kind == "gather":
                    dve.wait_ge(b_weighed, QT * b if j else QT * b + 1)
                    ins = dve.tensor_reduce(b_s[:, par ^ j, j, :], b_w8[:, j, :, :, :].rearrange("p h e s -> p (h e) s"),
                                            X_AXIS, ALU.add)
                    if j == 1:
                        link(ins)
                    else:
                        ins.then_inc(b_gathered, 1)
                elif kind == "expand":
                    dve.tensor_tensor(b_o[:, :, :, :].rearrange("p t h e -> p (t h) e"),
                                      b_s[:, 1 - par, :, :].rearrange("p t (h e) -> p (t h) e", e=EB),
                                      b_rs[:, 1 - par, :, :].rearrange("p t h -> p (t h)").unsqueeze(2)
                                      .to_broadcast([128, QT * H, EB]), ALU.mult).then_inc(b_normal, 1)
                elif kind == "project":
                    dve.wait_ge(b_filled, fill.count)
                    for t in range(QT):
                        for m in range(QT):
                            xb = X[64 * t:64 * t + 64, bass.ds((b - 1) * QT + m, 1), :].rearrange("p a d -> p (a d)")
                            ins = dve.tensor_tensor(xb, R[fill.bank][64 * m:64 * m + 64, t * 128:(t + 1) * 128], xb,
                                                    ALU.add)
                    ins.then_inc(b_added, 1)
            run_plan(dve, B_PLAN, do, chain, 2 * 6)
            dve.wait_ge(b_added, NB)

        def b_gpsimd(pool, chain):
            def do(step, i, fill):
                kind, par, j = step
                b = 2 * i + par
                if kind == "norm":
                    pool.wait_ge(b_stats, b + 3)
                    norm_rstd(pool, chain.link, QT).then_inc(b_rstd, 1)
                elif kind == "weigh":
                    if j == 0:
                        pool.wait_ge(b_exped, b + 1)
                        pool.wait_ge(b_values, b + 1)
                        wait(pool, b_gathered, b)
                    else:
                        wait(pool, b_normal, b)
                    for h in range(0 if j else HV, H):
                        ins = pool.tensor_tensor(b_w8[:, j, h, :, :],
                                                 b_v[:, par, j, h:h + H, :].rearrange("p s e -> p e s"),
                                                 b_e[:, par, j, :, h].unsqueeze(1).to_broadcast([128, EB, H]), ALU.mult)
                    ins.then_inc(b_weighed, 1)
            run_plan(pool, B_PLAN, do, chain, 2)

        f = {n: sem("f_" + n) for n in (
            "stats", "rstd", "normed", "xt_mm", "xt_ev", "h_mm", "gelu", "logit_mm", "shifted", "logit_exp",
            "alpha", "alt_mm", "alt_ev", "si_mm", "si", "sit_mm", "sit", "gi_mm", "gates", "gates_tanh", "n_in",
            "n_tanh", "new", "qkv_mm", "q", "kv", "score_mm", "score", "score_exp", "prob", "pt_mm", "pt", "y_mm",
            "y", "yt_mm", "yt", "so_mm", "so", "out_mm", "added")}
        f["ystats"] = sem("f_ystats")
        f["yrstd"] = sem("f_yrstd")
        OUT_BANKS = (6, 7, 0, 1)

        def f_order(t):
            b, q = divmod(t, QT)
            return (b // 2) * 4 + q * 2 + b % 2

        def f_tensor(pe, rep):
            with pe.Fori(0, CHUNKS) as c:
                k = c + rep * CHUNKS + 1
                pe.wait_ge(f["normed"], k)
                for n in range(CT // 4):
                    if n >= 2:
                        pe.wait_ge(f["xt_ev"], (k - 1) * 4 + n - 1)
                    for t in range(4):
                        ins = pe.transpose(PS[n % 2][:, t * 128:(t + 1) * 128], f_xs[:, 4 * n + t, 0:D], ident[:, :])
                    ins.then_inc(f["xt_mm"], 1)
                for n in range(CT // 4):
                    pe.wait_ge(f["xt_ev"], (k - 1) * 4 + n + 1)
                    pe.matmul(PS[2 + n][0:DH, :], w["w1a"][:, :], f_xt[:, n * 512:(n + 1) * 512],
                              start=True, stop=True).then_inc(f["h_mm"], 1)
                for t in range(CT):
                    if t % 4 == 0:
                        pe.wait_ge(f["gelu"], (k - 1) * 4 + t // 4 + 1)
                    o = f_order(t)
                    ins = pe.matmul(PS[6 + o // 8][:, (o % 8) * NS:(o % 8 + 1) * NS], f_h[:, t * 128:(t + 1) * 128],
                                    w2s[:, :], start=True, stop=True)
                ins.then_inc(f["logit_mm"], 1)
                pe.wait_ge(f["alpha"], k)
                for p in range(PAIRS):
                    for par in range(2):
                        for q in range(QT):
                            ins = pe.matmul(PS[4 + p // 2][64 * par:64 * par + 64, (p % 2) * 129:(p % 2) * 129 + 129],
                                            f_al[:, 4 * p + 2 * q + par, :], f_xs[:, 4 * p + 2 * par + q, :],
                                            start=q == 0, stop=q == QT - 1)
                ins.then_inc(f["si_mm"], 1)
                for n in range(CT // 2):
                    ins = pe.transpose(PS[n // 4][:, (n % 4) * 128:(n % 4 + 1) * 128],
                                       f_al[:, 2 * n:2 * n + 2, :].rearrange("p a s -> p (a s)"), ident[:, :])
                ins.then_inc(f["alt_mm"], 1)
                pe.wait_ge(f["si"], k)
                for p in range(PAIRS):
                    ins = pe.transpose(PS[2][:, p * 128:(p + 1) * 128], f_si[:, p, :], ident[:, :])
                ins.then_inc(f["sit_mm"], 1)
                pe.wait_ge(f["sit"], k)
                for n in range(3):
                    ins = pe.matmul(PS[3 + n][:, :], w["wih_t"][:, n * 128:(n + 1) * 128], f_sit[:, :],
                                    start=True, stop=True)
                ins.then_inc(f["gi_mm"], 1)
                pe.wait_ge(f["new"], k)
                pe.matmul(PS[6][0:DQ, :], w["wq"][:, :], f_sn[:, :], start=True, stop=True)
                pe.matmul(PS[7][0:DQ, :], w["wk"][:, :], f_sn[:, :], start=True, stop=True)
                for p in range(PAIRS):
                    pe.matmul(PS[2][:, p * 128:(p + 1) * 128], f_sn[:, p * 128:(p + 1) * 128], w["wv"][:, :],
                              start=True, stop=False)
                    ins = pe.matmul(PS[2][:, p * 128:(p + 1) * 128], ones[0:1, :], w["bv"][:, :],
                                    start=False, stop=True)
                ins.then_inc(f["qkv_mm"], 1)
                pe.wait_ge(f["q"], k)
                pe.wait_ge(f["kv"], k)
                pe.wait_ge(f["alt_ev"], k)
                for p in range(PAIRS):
                    for par in range(2):
                        sl = slice(p * 128 + par * 64, p * 128 + par * 64 + 64)
                        ins = pe.matmul(PS[0][64 * par:64 * par + 64, p * NS:(p + 1) * NS], f_q[:, sl], f_k[:, sl],
                                        start=True, stop=True)
                ins.then_inc(f["score_mm"], 1)
                pe.wait_ge(f["prob"], k)
                for p in range(PAIRS):
                    ins = pe.transpose(PS[1][:, p * 128:(p + 1) * 128], f_p[:, p, :], ident[:, :])
                ins.then_inc(f["pt_mm"], 1)
                pe.wait_ge(f["pt"], k)
                for p in range(PAIRS):
                    sl = slice(p * 128, (p + 1) * 128)
                    pe.matmul(PS[3][:, sl], f_pt[:, sl], f_v[:, p, :], start=True, stop=False)
                    ins = pe.matmul(PS[3][:, sl], f_sn[:, sl], ident[:, :], start=False, stop=True)
                ins.then_inc(f["y_mm"], 1)
                pe.wait_ge(f["y"], k)
                for p in range(PAIRS):
                    ins = pe.transpose(PS[4][:, p * 128:(p + 1) * 128], f_y[:, p, :], ident[:, :])
                ins.then_inc(f["yt_mm"], 1)
                pe.wait_ge(f["yt"], k)
                for p in range(PAIRS):
                    sl = slice(p * 128, (p + 1) * 128)
                    pe.matmul(PS[5][:, sl], f_yt[:, sl], wcomb[:, :], start=True, stop=False)
                    ins = pe.matmul(PS[5][:, sl], ones[0:1, :], crow[:, :], start=False, stop=True)
                ins.then_inc(f["so_mm"], 1)
                pe.wait_ge(f["so"], k)
                for n in range(4):
                    pp, par = divmod(n, 2)
                    for m in range(4):
                        p, q = 2 * pp + m // 2, m % 2
                        ins = pe.matmul(PS[OUT_BANKS[n]][:, m * 128:(m + 1) * 128],
                                        f_alt[64 * par:64 * par + 64, 2 * p + q, :],
                                        f_so[64 * par:64 * par + 64, p, :], start=True, stop=True)
                    ins.then_inc(f["out_mm"], 1)

        def f_scalar(act, rep):
            with act.Fori(0, CHUNKS) as c:
                k = c + rep * CHUNKS + 1
                for n in range(CT // 4):
                    act.wait_ge(f["xt_mm"], (k - 1) * 4 + n + 1)
                    act.activation(f_xt[:, n * 512:(n + 1) * 512], PS[n % 2][:, :], ACT.Copy).then_inc(f["xt_ev"], 1)
                for n in range(CT // 4):
                    act.wait_ge(f["h_mm"], (k - 1) * 4 + n + 1)
                    act.activation(f_h[0:DH, n * 512:(n + 1) * 512], PS[2 + n][0:DH, :], ACT.Gelu,
                                   bias=c1[:, :]).then_inc(f["gelu"], 1)
                act.wait_ge(f["shifted"], k)
                act.activation(f_e[:, :, :], f_e[:, :, :], ACT.Exp).then_inc(f["logit_exp"], 1)
                act.wait_ge(f["alt_mm"], k)
                for n in range(2):
                    ins = act.activation(f_alt[:, 4 * n:4 * n + 4, :].rearrange("p a s -> p (a s)"), PS[n][:, :], ACT.Copy)
                ins.then_inc(f["alt_ev"], 1)
                act.wait_ge(f["sit_mm"], k)
                act.activation(f_sit[:, :], PS[2][:, :], ACT.Copy).then_inc(f["sit"], 1)
                act.wait_ge(f["gates"], k)
                act.activation(f_r[:, :], f_r[:, :], ACT.Tanh, scale=0.5)
                act.activation(f_zg[:, :], f_zg[:, :], ACT.Tanh, scale=0.5).then_inc(f["gates_tanh"], 1)
                act.wait_ge(f["n_in"], k)
                act.activation(f_n[:, :], f_n[:, :], ACT.Tanh, bias=w["bih"][:, 2:3]).then_inc(f["n_tanh"], 1)
                act.wait_ge(f["qkv_mm"], k)
                act.activation(f_q[:, :], PS[6][0:DQ, :], ACT.Identity, bias=w["bq"][:, :]).then_inc(f["q"], 1)
                act.wait_ge(f["score"], k)
                act.activation(f_s[:, :, :], f_s[:, :, :], ACT.Exp, scale=DQ ** -0.5).then_inc(f["score_exp"], 1)
                act.wait_ge(f["pt_mm"], k)
                act.activation(f_pt[:, :], PS[1][:, :], ACT.Copy).then_inc(f["pt"], 1)
                act.wait_ge(f["yt_mm"], k)
                act.activation(f_yt[:, :], PS[4][:, :], ACT.Copy).then_inc(f["yt"], 1)
                act.wait_ge(f["so_mm"], k)
                act.activation(f_so[:, :, :].rearrange("p a d -> p (a d)"), PS[5][:, :], ACT.Copy).then_inc(f["so"], 1)

        def f_vector(dve, rep, chain):
            link = chain.link
            x = X

            def pairs(ap):
                return ap.rearrange("p (a d) -> p a d", a=PAIRS)

            with dve.Fori(0, CHUNKS) as c:
                chain.enter(c, 15)
                k = c + rep * CHUNKS + 1
                norm_stats(dve, link, x, c * CT, CT).then_inc(f["stats"], 1)
                dve.wait_ge(f["rstd"], k)
                norm_apply(dve, x, c * CT, CT, f_xs).then_inc(f["normed"], 1)
                dve.wait_ge(f["logit_mm"], k)
                dve.memset(gate[:, :], 0.0)
                for t in range(CT):
                    ins = dve.max(f_v8[:, t, :], PS[6 + t // 8][:, (t % 8) * NS:(t % 8 + 1) * NS])
                link(ins)
                for n in range(2):
                    ins = dve.tensor_tensor(f_e[:, 8 * n:8 * n + 8, :], PS[6 + n][:, :].rearrange("p (t s) -> p t s", t=8),
                                            f_v8[:, 8 * n:8 * n + 8, 0:1].to_broadcast([128, 8, NS]), ALU.subtract)
                ins.then_inc(f["shifted"], 1)
                for t in range(CT):
                    ins = dve.match_replace(f_z[:, t, :], f_v8[:, t, :], PS[6 + t // 8][:, (t % 8) * NS:(t % 8 + 1) * NS],
                                            TAKEN)
                link(ins)
                dve.wait_ge(f["logit_exp"], k)
                link(dve.scalar_tensor_tensor(f_al[:, :, :], f_z[:, :, :], TAKEN, f_e[:, :, :], ALU.is_equal, ALU.mult))
                link(dve.tensor_reduce(f_sum[:, :], f_al[:, :, :], X_AXIS, ALU.add))
                link(dve.reciprocal(f_sum[:, :], f_sum[:, :]))
                dve.tensor_tensor(f_al[:, :, :], f_al[:, :, :], f_sum[:, :].unsqueeze(2).to_broadcast([128, CT, NS]),
                                  ALU.mult).then_inc(f["alpha"], 1)
                dve.wait_ge(f["si_mm"], k)
                for n in range(2):
                    si = PS[4 + n][:, 0:258].rearrange("p (a d) -> p a d", a=2)
                    ins = dve.tensor_scalar(f_den[:, 2 * n:2 * n + 2], si[:, :, D:D + 1].rearrange("p a d -> p (a d)"),
                                            1e-8, None, ALU.add)
                link(ins)
                link(dve.reciprocal(f_den[:, :], f_den[:, :]))
                for n in range(2):
                    si = PS[4 + n][:, 0:258].rearrange("p (a d) -> p a d", a=2)
                    ins = dve.tensor_tensor(f_si[:, 2 * n:2 * n + 2, :], si[:, :, 0:D],
                                            f_den[:, 2 * n:2 * n + 2].unsqueeze(2).to_broadcast([128, 2, D]), ALU.mult)
                ins.then_inc(f["si"], 1)
                dve.wait_ge(f["gi_mm"], k)
                for n, dst in ((0, f_r), (1, f_zg)):
                    ins = dve.tensor_tensor(dst[:, :].rearrange("p (b s) -> p b s", s=NS),
                                            PS[3 + n][:, :].rearrange("p (b s) -> p b s", s=NS),
                                            gate_h[:, n:n + 1, :].to_broadcast([128, CB, NS]), ALU.add)
                ins.then_inc(f["gates"], 1)
                dve.wait_ge(f["gates_tanh"], k)
                link(dve.scalar_tensor_tensor(f_t[:, :].rearrange("p (b s) -> p b s", s=NS),
                                              f_r[:, :].rearrange("p (b s) -> p b s", s=NS), 1.0,
                                              hn_half[:, :].unsqueeze(1).to_broadcast([128, CB, NS]), ALU.add, ALU.mult))
                dve.tensor_tensor(f_n[:, :], PS[5][:, :], f_t[:, :], ALU.add).then_inc(f["n_in"], 1)
                dve.wait_ge(f["n_tanh"], k)
                link(dve.tensor_tensor(f_t[:, :].rearrange("p (b s) -> p b s", s=NS),
                                       w["slot_t"][:, :].unsqueeze(1).to_broadcast([128, CB, NS]),
                                       f_n[:, :].rearrange("p (b s) -> p b s", s=NS), ALU.subtract))
                link(dve.scalar_tensor_tensor(f_zg[:, :], f_zg[:, :], 1.0, f_t[:, :], ALU.add, ALU.mult))
                dve.scalar_tensor_tensor(f_sn[:, :], f_zg[:, :], 0.5, f_n[:, :], ALU.mult, ALU.add).then_inc(f["new"], 1)
                dve.wait_ge(f["qkv_mm"], k)
                dve.tensor_scalar(f_k[:, :], PS[7][0:DQ, :], w["bk"][:, :], None, ALU.add)
                dve.tensor_copy(f_v[:, :, :], pairs(PS[2][:, :])).then_inc(f["kv"], 1)
                dve.wait_ge(f["score_mm"], k)
                sc = PS[0][:, 0:PAIRS * NS].rearrange("p (a s) -> p a s", a=PAIRS)
                link(dve.tensor_reduce(f_m[:, :], sc, X_AXIS, ALU.max))
                dve.tensor_tensor(f_s[:, :, :], sc, f_m[:, :].unsqueeze(2).to_broadcast([128, PAIRS, NS]),
                                  ALU.subtract).then_inc(f["score"], 1)
                dve.wait_ge(f["score_exp"], k)
                link(dve.tensor_reduce(f_rs[:, :], f_s[:, :, :], X_AXIS, ALU.add))
                link(dve.reciprocal(f_rs[:, :], f_rs[:, :]))
                for par in range(2):
                    p = slice(64 * par, 64 * par + 64)
                    ins = dve.tensor_tensor(f_p[p, :, par * NS:(par + 1) * NS], f_s[p, :, :],
                                            f_rs[p, :].unsqueeze(2).to_broadcast([64, PAIRS, NS]), ALU.mult)
                ins.then_inc(f["prob"], 1)
                dve.wait_ge(f["y_mm"], k)
                y = pairs(PS[3][:, :])
                for p in range(PAIRS):
                    ins = dve.bn_stats(stats[:, p, :], y[:, p, :])
                link(ins)
                dve.memset(gate[:, :], 0.0)
                for p in range(PAIRS):
                    ins = dve.bn_aggr(mv[:, p, :], stats[:, p, :])
                ins.then_inc(f["ystats"], 1)
                dve.wait_ge(f["yrstd"], k)
                for p in range(PAIRS):
                    ins = dve.tensor_scalar(f_y[:, p, :], y[:, p, :], mv[:, p, 0:1], rstd[:, p:p + 1],
                                            ALU.subtract, ALU.mult)
                ins.then_inc(f["y"], 1)
                for n in range(4):
                    pp, par = divmod(n, 2)
                    dve.wait_ge(f["out_mm"], (k - 1) * 4 + n + 1)
                    xs = x[:, bass.ds(c * CT + 8 * pp, 8), :].rearrange("p (a r q) d -> p a r (q d)", a=2, r=2)[:, :, par, :]
                    dve.tensor_tensor(xs, PS[OUT_BANKS[n]][:, :].rearrange("p (a e) -> p a e", a=2), xs,
                                      ALU.add).then_inc(f["added"], 1)
            chain.leave(CHUNKS)
            dve.wait_ge(f["added"], (rep + 1) * CHUNKS * (CT // 4))

        def f_gpsimd(pool, rep, chain):
            with pool.Fori(0, CHUNKS) as c:
                chain.enter(c, 2)
                k = c + rep * CHUNKS + 1
                pool.wait_ge(f["stats"], k)
                norm_rstd(pool, chain.link, CT).then_inc(f["rstd"], 1)
                pool.wait_ge(f["ystats"], k)
                norm_rstd(pool, chain.link, PAIRS).then_inc(f["yrstd"], 1)
            chain.leave(CHUNKS)

        block = ctx.enter_context(nc.Block())

        @block.sync
        def _(sp):
            for n in range(2):
                sp.dma_start(X[:, n * CT:(n + 1) * CT, :], x_in[:, n * CT:(n + 1) * CT, :]).then_inc(x_loaded, 16)
            for n in WEIGHTS:
                sp.dma_start(w[n][:], w_in[n]).then_inc(w_loaded, 16)
            for c in range(CHUNKS):
                sp.wait_ge(f["added"], (CHUNKS + c + 1) * 4)
                sp.dma_start(out[:, c * CT:(c + 1) * CT, :], X[:, c * CT:(c + 1) * CT, :]).then_inc(stored, 16)
            sp.wait_ge(stored, 16 * CHUNKS)

        @block.gpsimd
        def _(pool):
            chain = Chain(pool, pool_chain)
            pool.memset(minus_half[:, :], -0.5)
            pool.memset(eps[:, :], EPS)
            pool.memset(ones[:, :], 1.0)
            pool.memset(a_v[:, :, :, :, EA:W], 1.0)
            pool.memset(f_p[:, :, :], 0.0)
            pool.memset(f_xs[:, :, D:D + 1], 1.0).then_inc(pool_set, 1)
            pool.wait_ge(pool_set, 1)
            pool.wait_ge(x_loaded, 32)
            a_gpsimd(pool, chain)
            f_gpsimd(pool, 0, chain)
            b_gpsimd(pool, chain)
            f_gpsimd(pool, 1, chain)

        @block.scalar
        def _(act):
            act.wait_ge(dve_set, 1)
            a_scalar(act)
            f_scalar(act, 0)
            b_scalar(act)
            f_scalar(act, 1)

        @block.vector
        def _(dve):
            chain = Chain(dve, dve_chain)
            link = chain.link
            dve.memset(f_h[DH:DH + 1, :], 1.0)
            dve.wait_ge(w_loaded, 16 * len(WEIGHTS))
            dve.wait_ge(x_loaded, 32)
            dve.wait_ge(pool_set, 1)
            dve.tensor_copy(a_wqk_h[:, :, :, :], w["a_wqk"][:, :, :, :])
            dve.tensor_scalar(a_wv_h[:, :], w["a_wv"][:, :], V_UP, None, ALU.mult)
            link(dve.tensor_copy(b_w_h[:, :, :], w["b_wqkv"][:, :, :]))
            dve.tensor_tensor(a_wqk_l[:, :, :, :], w["a_wqk"][:, :, :, :], a_wqk_h[:, :, :, :], ALU.subtract)
            dve.scalar_tensor_tensor(a_wv_l[:, :], w["a_wv"][:, :], V_UP, a_wv_h[:, :], ALU.mult, ALU.subtract)
            dve.tensor_tensor(b_w_l[:, :, :], w["b_wqkv"][:, :, :], b_w_h[:, :, :], ALU.subtract)
            link(dve.scalar_tensor_tensor(inv_tau[:, 0:1], w["tau"][:, :], -1.0, w["tau"][:, :], ALU.mult, ALU.max))
            link(dve.tensor_scalar(inv_tau[:, 0:1], inv_tau[:, 0:1], 0.1, None, ALU.add))
            link(dve.reciprocal(inv_tau[:, 1:2], inv_tau[:, 0:1]))
            dve.tensor_scalar(w2s[:, :], w["w2b"][:, :], inv_tau[:, 1:2], None, ALU.mult)
            link(dve.tensor_tensor(brz[:, :], w["bih"][:, 0:2], w["bhh"][:, 0:2], ALU.add))
            dve.wait_ge(set_mm, 1)
            for n in range(2):
                dve.tensor_scalar(gate_h[:, n, :], PS[0][:, n * NS:(n + 1) * NS], brz[:, n:n + 1], None, ALU.add)
            dve.tensor_scalar(hn_half[:, :], PS[0][:, 2 * NS:3 * NS], w["bhh"][:, 2:3], 0.5, ALU.add, ALU.mult)
            dve.tensor_scalar(slot_mean[:, :], PS[1][:, 0:1], 1.0 / NS, None, ALU.mult)
            dve.tensor_tensor(cmid[:, :], PS[2][:, 0:1], w["bvp"][:, :], ALU.add)
            dve.tensor_scalar(wcomb[:, :], PS[3][:, 0:128], w["ln_g"][:, :], None, ALU.mult).then_inc(set_ev, 1)
            dve.wait_ge(set_mm, 2)
            dve.tensor_tensor(c1[:, :], PS[4][0:DH, 0:1], w["b1"][:, :], ALU.add)
            dve.tensor_tensor(crow[:, :], PS[5][0:1, 0:128], w["bo"][:, :], ALU.add).then_inc(dve_set, 1)
            dve.wait_ge(dve_set, 1)
            a_vector(dve, chain)
            f_vector(dve, 0, chain)
            b_vector(dve, chain)
            f_vector(dve, 1, chain)

        @block.tensor
        def _(pe):
            pe.wait_ge(pool_set, 1)
            pe.wait_ge(w_loaded, 16 * len(WEIGHTS))
            for n in range(3):
                pe.matmul(PS[0][:, n * NS:(n + 1) * NS], w["whh_t"][:, n * 128:(n + 1) * 128], w["slot_t"][:, :],
                          start=True, stop=True)
            pe.matmul(PS[1][:, 0:1], w["slot"][:, :], ones[0:NS, 0:1], start=True, stop=True)
            pe.matmul(PS[2][:, 0:1], w["wvp"][:, :], w["ln_b"][:, :], start=True, stop=True)
            pe.matmul(PS[3][:, 0:128], w["wvp_t"][:, :], w["wo"][:, :], start=True, stop=True).then_inc(set_mm, 1)
            pe.wait_ge(set_ev, 1)
            pe.matmul(PS[4][0:DH, 0:1], w["w1b"][:, :], slot_mean[:, :], start=True, stop=True)
            pe.matmul(PS[5][0:1, 0:128], cmid[:, :], w["wo"][:, :], start=True, stop=True).then_inc(set_mm, 1)
            pe.wait_ge(dve_set, 1)
            a_tensor(pe)
            f_tensor(pe, 0)
            b_tensor(pe)
            f_tensor(pe, 1)


def token_of_partition():
    return np.array([16 * h + 8 * t + r for t in range(2) for h in range(8) for r in range(8)])


def constants():
    bf16 = mybir.dt.np(BF16)
    row = token_of_partition()
    later = np.where(row[None, :] > row[:, None], MASKED, 0.0)
    roll = np.zeros((128, H, 128), np.float16)
    for n in range(H):
        for h in range(H):
            for e in range(EB):
                roll[EB * ((h + n) % H) + e, n, EB * h + e] = 1.0
    heads = np.repeat(np.eye(H, dtype=np.float32), EB, axis=0)
    rowmask = (row[:, None] // H == np.arange(TB)[None, :]).astype(np.float32)
    onehot = np.zeros((4, 4, 128), np.float32)
    for h in range(4):
        onehot[h, h, :] = 1.0
    return {
        "ident": np.eye(128, dtype=np.float32), "identb": np.eye(128).astype(bf16),
        "onehot": onehot.astype(bf16), "roll": roll, "heads": heads, "rowmask": rowmask,
        "mask_q": np.repeat(later[:, None, :], 4, 1).astype(bf16),
        "mask_k": np.repeat(later.T[:, None, :], 4, 1).astype(bf16),
    }


def kernel(**inputs):
    import concourse.bacc as bacc
    from concourse.bass_utils import run_bass_kernel_spmd

    def get(name):
        return np.asarray(inputs[name])

    def ffn(name):
        return get("L0_ffn_" + name)

    def column(v):
        return v.reshape(-1, 1)

    def flat_t(v):
        return v.reshape(H * EA, D).T

    wq, wk = (flat_t(get("L0_attn_a_w" + n)).reshape(D, 8, 1, 128) for n in "qk")
    arrays = constants()
    arrays.update({
        "a_wqk": np.concatenate([wq, wk], axis=2), "a_wv": flat_t(get("L0_attn_a_wv")),
        "a_wo": get("L0_attn_a_wo").T.reshape(8, 128, D).transpose(1, 0, 2),
        "b_wqkv": np.stack([get("L0_attn_b_W" + n).T for n in "qkv"], axis=1),
        "b_wo": get("L0_attn_b_Wo").T.reshape(H, EB, D)[token_of_partition() % H], "b_bo": get("L0_attn_b_bo").reshape(1, D),
        "slot": ffn("slot_init"), "slot_t": ffn("slot_init").T,
        "w1a": ffn("w1")[:D], "w1b": ffn("w1")[D:], "b1": column(ffn("b1")),
        "w2b": np.concatenate([ffn("w2"), ffn("b2").reshape(1, NS)]),
        "tau": np.broadcast_to(ffn("tau").reshape(1, 1), (NS + 1, 1)),
        "wih_t": ffn("Wih").T, "whh_t": ffn("Whh").T,
        "bih": ffn("bih").reshape(3, D).T, "bhh": ffn("bhh").reshape(3, D).T,
        "wq": ffn("wq"), "bq": column(ffn("bq")), "wk": ffn("wk"), "bk": column(ffn("bk")),
        "wv": ffn("wv"), "bv": ffn("bv").reshape(1, D),
        "ln_g": column(ffn("ln_g")), "ln_b": column(ffn("ln_b")),
        "wvp": ffn("wvp"), "wvp_t": ffn("wvp").T, "bvp": column(ffn("bvp")),
        "wo": ffn("wo"), "bo": ffn("bo").reshape(1, D),
    })
    place = token_of_partition()
    x = get("L0_attn_a_x")
    shape = x.shape
    x = x.reshape(NT, 128, D)[:, place, :].transpose(1, 0, 2)
    nc = bacc.Bacc("TRN2", target_bir_lowering=False, num_devices=1)
    feeds = {"x_dram": np.ascontiguousarray(x)}
    x_in = nc.dram_tensor("x_dram", list(x.shape), F32, kind="ExternalInput").ap()
    w_in = {}
    for name in WEIGHTS:
        a = np.ascontiguousarray(arrays[name])
        feeds[name + "_dram"] = a
        w_in[name] = nc.dram_tensor(name + "_dram", list(a.shape), mybir.dt.from_np(a.dtype), kind="ExternalInput").ap()
    out = nc.dram_tensor("out_dram", list(x.shape), F32, kind="ExternalOutput").ap()
    build(nc, x_in, w_in, out)
    result = run_bass_kernel_spmd(nc, [feeds], core_ids=[0]).results[0]["out_dram"]
    y = np.empty((NT, 128, D), result.dtype)
    y[:, place, :] = result.transpose(1, 0, 2)
    return y.reshape(shape)
```

```python
import concourse.bass as bass
from concourse import mybir
from contextlib import ExitStack
import numpy as np

F32 = mybir.dt.float32
F16 = mybir.dt.float16
BF16 = mybir.dt.bfloat16
ACT = mybir.ActivationFunctionType
ALU = mybir.AluOpType
X_AXIS = mybir.AxisListType.X

NB, SEQ, D = 16, 256, 128
NT = NB * SEQ // 128
QT = SEQ // 128
H = 16
EA = 64
EB = D // H
GA = H // 4
NS, TOPK, DQ, DH = 64, 8, D // 4, D // 2
EPS = 1e-5
V_UP = 32.0
CHUNKS = 2
CB = NB // CHUNKS
CT = CB * QT
PAIRS = CB // 2
MASKED = -1e30
LARGEST = 3e38
TAKEN = -3e38
W = EA + 1
ROLLS = H // 2
HV = 9
TB = 8


class Chain:

    def __init__(self, eng, sem):
        self.eng, self.sem, self.count, self.looped = eng, sem, 0, 0

    def link(self, ins):
        self.count += 1
        ins.then_inc(self.sem, 1)
        self.eng.wait_ge(self.sem, self.looped + self.count)

    def enter(self, trip, per):
        self.looped, self.before, self.per = trip * per, self.count, per

    def leave(self, trips):
        assert self.count - self.before == self.per, (self.count - self.before, self.per)
        self.looped, self.count = 0, self.before + trips * self.per



def a_steps(first=False, last=False):
    steps = []
    for g in range(GA):
        prepare = not (last and g == GA - 1)

        def put(cond, *new):
            steps.extend((kind, g, n) for kind, n in new if cond)
        put(True, ("exps", 0))
        put(prepare, ("qk", 0))
        put(True, ("exps", 1))
        put(prepare, ("qk", 1))
        put(True, ("mask", 0), ("exps", 2), ("mask", 1))
        put(g == 1 and not first, ("project", 0))
        put(prepare, ("max", 0), ("v", 0))
        put(True, ("mask", 2))
        put(prepare, ("max", 1))
        put(True, ("pv", 0))
        put(prepare, ("max", 2))
        put(True, ("pv", 1))
        put(not (first and g == 0), ("turn", 0))
        put(g == 1 and not last, ("norm", 0))
        put(g == 2 and not last, ("apply", 0), ("xt", 0))
        put(prepare, ("maxrow", 0))
        put(True, ("normal", 0))
        put(last and g == 2, ("ffn_stats", 0))
        put(last and g == 3, ("ffn_apply", 0))
    return steps


def b_steps(par, former=True, before=True, ahead=True, ahead2=True):
    one, two = ahead, ahead2
    steps = []

    def put(cond, *names):
        if cond:
            steps.extend((n[0], par, n[1]) if isinstance(n, tuple) else (n, par, 0) for n in names)
    put(True, "soft")
    put(one, "v", ("roll", 0), ("roll", 1))
    put(before, "project")
    put(former, ("gather", 1))
    put(one, ("roll", 2))
    put(before, ("projects", 1))
    put(former, "normal")
    put(one, ("roll", 3))
    put(True, "sumexp")
    put(before, ("projects", 2))
    put(one, ("roll", 4))
    put(former, "expand")
    put(True, ("weigh", 0), ("weigh", 1))
    put(before, ("projects", 3))
    put(one, ("dots", 0), ("roll", 5))
    put(before, "add")
    put(two, "norm")
    put(True, ("weigh", 2))
    put(one, ("roll", 6), ("flip", 0))
    put(two, "apply")
    put(one, ("roll", 7))
    put(two, "xt")
    put(one, ("dots", 1))
    put(True, ("gather", 0))
    put(two, "qk")
    put(one, ("flip", 1))
    return steps


A_PROLOGUE = [("norm", 3, 0), ("apply", 3, 0), ("xt", 3, 0), ("qk", 3, 0), ("qk", 3, 1), ("v", 3, 0),
              ("max", 3, 0), ("max", 3, 1), ("max", 3, 2), ("maxrow", 3, 0)]
A_EPILOGUE = [("turn", 0, 0), ("project", 0, 0)]
B_PROLOGUE = [("norm", 0, 0), ("apply", 0, 0), ("xt", 0, 0), ("qk", 0, 0), ("v", 1, 0)]
for m in range(ROLLS):
    B_PROLOGUE += [("roll", 1, m)] + ([("dots", 1, m // 4)] if m % 4 == 3 else [])
B_PROLOGUE += [("flip", 1, 0), ("flip", 1, 1), ("norm", 1, 0), ("apply", 1, 0), ("xt", 1, 0), ("qk", 1, 0)]
B_EPILOGUE = ([("project", 0, 0)] + [("projects", 0, m) for m in range(1, 4)] +
              [("gather", 0, 1), ("normal", 0, 0), ("ffn_stats", 0, 0), ("add", 0, 0), ("expand", 0, 0),
               ("ffn_apply", 0, 0), ("project", 1, 0)] + [("projects", 1, m) for m in range(1, 4)] + [("add", 1, 0)])

R_STEPS = ("qk", "v", "turn", "project", "xt", "maxrow")


def fills_of(steps):
    return [s for s in steps if s[0] in R_STEPS]


A_PLAN = [(A_PROLOGUE, -1, None), (a_steps(first=True), 0, None), (a_steps(), 1, NB - 2),
          (a_steps(last=True), NB - 1, None), (A_EPILOGUE, NB, None)]
B_PLAN = [(B_PROLOGUE, -1, None), (b_steps(0, former=False, before=False) + b_steps(1, before=False), 0, None),
          (b_steps(0) + b_steps(1), 1, NB // 2 - 2),
          (b_steps(0, ahead2=False) + b_steps(1, ahead=False, ahead2=False), NB // 2 - 1, None),
          (B_EPILOGUE, NB // 2, None)]


F_PLAN = [("stats", 1), ("hidden", 0), ("apply", 1), ("logits", 0), ("hidden", 1),
          ("logits", 1), ("top", 0), ("alpha", 0), ("read", 0), ("top", 1), ("slots", 0), ("inputs", 0), ("alpha", 1),
          ("read", 1), ("gates", 0), ("slots", 1), ("inputs", 1)]
LATER = ["gates", "candidate", "new", "qkv", "scores", "probs", "attend", "ynorm", "values", "out"]
F_PLAN.append(("candidate", 0))
for n in range(2, len(LATER) + 2):
    F_PLAN += [(LATER[m], c) for m, c in ((n, 0), (n - 2, 1)) if m < len(LATER)]


class Fill:

    def __init__(self, number, looped, former):
        self.bank, self.count, self.former = number % 2, number + 1 + looped, former


def run_plan(eng, plan, do, chain=None, per=0):
    number, history = 0, []
    for steps, index, trips in plan:
        mine = fills_of(steps)
        if trips:
            assert len(mine) % 2 == 0 and [f[0] for f in history[-2:]] == mine[-2:]
            with eng.Fori(0, trips) as i:
                if chain:
                    chain.enter(i, per)
                past, k = [(f, index - 1 + i) for f in mine[-2:]], 0
                for step in steps:
                    fill = None
                    if step[0] in R_STEPS:
                        fill = Fill(number + k, i * len(mine), past[-2])
                        past.append((step, index + i))
                        k += 1
                    do(step, index + i, fill)
            if chain:
                chain.leave(trips)
            history += [(f, index + trips - 1) for f in mine]
            number += trips * len(mine)
        else:
            for step in steps:
                fill = None
                if step[0] in R_STEPS:
                    fill = Fill(number, 0, history[-2] if len(history) >= 2 else None)
                    history.append((step, index))
                    number += 1
                do(step, index, fill)


PACK_NAMES = {
    "first": ["ident", "a_wqk", "a_wv"],
    "masks": ["identb", "mask_q", "onehot"],
    "limit": ["limit_k"],
    "rest": ["a_wo", "w2b", "tau", "w1a", "w1b", "b1", "slot", "slot_t", "wih_t", "whh_t", "bih", "bhh", "wq", "bq",
             "wk", "bk", "wv", "bv", "ln_g", "ln_b", "wvp", "wvp_t", "bvp", "wo", "bo", "heads", "rowmask", "b_wqkv",
             "b_wo", "b_bo"],
    "rolls": ["roll"],
}


def build(nc, x_in, w_in, shapes, out):
    ctx = ExitStack()
    with ctx:
        def sb(name, shape, dt=F32, stage=ctx):
            return stage.enter_context(nc.sbuf_tensor(name, shape, dt))

        def sem(name):
            return ctx.enter_context(nc.semaphore(name))

        packs = {n: sb("w_" + n, list(p.shape), p.dtype) for n, p in w_in.items()}
        w = {}
        for pack, tile in packs.items():
            column = 0
            for name in PACK_NAMES[pack]:
                shape = shapes[name]
                size = int(np.prod(shape[1:]))
                flat = tile[0:shape[0], column:column + size]
                w[name] = flat if len(shape) == 2 else flat.rearrange(
                    "p (a b) -> p a b" if len(shape) == 3 else "p (a b c) -> p a b c",
                    **dict(zip("ab", shape[1:-1])))
                column += size
        ident, identb = w["ident"], w["identb"]
        ones = sb("ones", [128, 128])
        a_wqk_h, a_wqk_l = sb("a_wqk_h", [128, 8, 2, 128], F16), sb("a_wqk_l", [128, 8, 2, 128], F16)
        a_wv_h, a_wv_l = sb("a_wv_h", [128, H * EA], F16), sb("a_wv_l", [128, H * EA], F16)
        b_w_h, b_w_l = sb("b_w_h", [128, 3, 128], F16), sb("b_w_l", [128, 3, 128], F16)
        w2s = sb("w2s", [NS + 1, NS])
        inv_tau = sb("inv_tau", [NS + 1, 2])
        slot_mean, c1 = sb("slot_mean", [128, 1]), sb("c1", [DH, 1])
        brz = sb("brz", [128, 2])
        gate_h, hn_half = sb("gate_h", [128, 2, NS]), sb("hn_half", [128, NS])
        cmid, wcomb, crow = sb("cmid", [128, 1]), sb("wcomb", [128, 128]), sb("crow", [1, 128])
        minus_half, eps = sb("minus_half", [128, CT]), sb("eps", [128, CT])

        X = sb("X", [128, NT, D])
        stats, mv = sb("stats", [128, NT, 6]), sb("mv", [128, NT, 2])
        veps, rstd = sb("veps", [128, NT]), sb("rstd", [128, NT])
        xn = sb("xn", [128, QT, D])
        gate = sb("gate", [128, 1])
        xh, xl = sb("xh", [128, SEQ], F16), sb("xl", [128, SEQ], F16)

        a_v = sb("a_v", [128, 2, QT, 4, W])
        f_h = sb("f_h", [DH + 1, CT * 128])
        f_xs = [sb(f"f_xs{c}", [128, CT, D + 1]) for c in range(CHUNKS)]
        f_p = [sb(f"f_p{c}", [128, PAIRS, 2 * NS]) for c in range(CHUNKS)]

        with ExitStack() as in_f:
            f_xt = sb("f_xt", [128, CT * 128], stage=in_f)
            f_v8 = sb("f_v8", [128, CT, TOPK], stage=in_f)
            f_z, f_e = sb("f_z", [128, CT, NS], stage=in_f), sb("f_e", [128, CT, NS], stage=in_f)
            f_sum = sb("f_sum", [128, CT], stage=in_f)
            CHUNK_BUFFERS = {
                "al": [128, CT, NS],
                "alt": [128, CT // 2, 128], "den": [128, PAIRS], "si": [128, PAIRS, D], "sit": [128, 512],
                "r": [128, 512], "zg": [128, 512], "n": [128, 512], "t": [128, 512],
                "sn": [128, 512],
                "q": [DQ, 512], "k": [DQ, 512], "v": [128, PAIRS, D], "m": [128, PAIRS], "rs": [128, PAIRS],
                "s": [128, PAIRS, NS], "pt": [128, 512], "y": [128, PAIRS, D], "yt": [128, 512],
                "so": [128, PAIRS, D]}
            chunk = [{name: sb(f"f_{name}{c}", shape, stage=in_f) for name, shape in CHUNK_BUFFERS.items()}
                     | {"xs": f_xs[c], "p": f_p[c]} for c in range(CHUNKS)]
        with ExitStack() as in_a:
            a_qk_h = sb("a_qk_h", [128, 2, 2, 2, SEQ], F16, stage=in_a)
            a_qk_l = sb("a_qk_l", [128, 2, 2, 2, SEQ], F16, stage=in_a)
            a_nm, a_nmt = sb("a_nm", [128, 2, QT, 4], BF16, stage=in_a), sb("a_nmt", [4, 2, SEQ], BF16, stage=in_a)
            a_p = sb("a_p", [128, 2, 3, 512], stage=in_a)
            a_rs = sb("a_rs", [128, QT, 4], stage=in_a)
            a_o = sb("a_o", [128, 2, QT, 4, EA], stage=in_a)
            a_ot = sb("a_ot", [128, 8, SEQ], stage=in_a)

        b_qt = sb("b_qt", [128, 2, SEQ])
        b_kh, b_kl = sb("b_kh", [128, 2, SEQ], F16), sb("b_kl", [128, 2, SEQ], F16)
        b_prod = sb("b_prod", [128, ROLLS, 2, SEQ])
        b_st = sb("b_st", [128, 2, 2 * SEQ])
        b_v = sb("b_v", [128, 2, QT, 2 * H, EB])
        b_e = sb("b_e", [128, 2, QT, H, H])
        b_m, b_rs = sb("b_m", [128, QT, H]), sb("b_rs", [128, 2, QT, H])
        b_w8 = sb("b_w8", [128, QT, H, EB, H])
        b_s = sb("b_s", [128, 2, QT, H * EB])
        b_o = sb("b_o", [128, QT, H, EB])
        b_ox = sb("b_ox", [128, 2, QT, EB, H, TB])

        PS = [ctx.enter_context(nc.psum_tensor(f"PS{i}", [128, 512], F32)) for i in range(8)]
        R, T, M, O = PS[0:2], PS[2:4], PS[4:6], PS[6:8]
        RB16 = [r[:, :].bitcast(BF16) for r in R]

        x_early, x_late, a_loaded, w_loaded = sem("x_early"), sem("x_late"), sem("a_loaded"), sem("w_loaded")
        stored = sem("stored")
        dve_chain, pool_chain = sem("dve_chain"), sem("pool_chain")
        pool_set, dve_set = sem("pool_set"), sem("dve_set")
        set_mm, set_ev, consts_set = sem("set_mm"), sem("set_ev"), sem("consts_set")

        def mm3(pe, dst, ah, al, bh, bl, start, stop):
            pe.matmul(dst, ah, bh, start=start, stop=False, skip_group_check=True)
            pe.matmul(dst, ah, bl, start=False, stop=False, skip_group_check=True)
            return pe.matmul(dst, al, bh, start=False, stop=stop, skip_group_check=True)

        def wait(eng, semaphore, value):
            if not (isinstance(value, int) and value <= 0):
                eng.wait_ge(semaphore, value)

        def one_tile(t):
            return slice(t, t + 1) if isinstance(t, int) else bass.ds(t, 1)

        def norm_stats(dve, link, X, tile, n, o=0):
            for t in range(n):
                ins = dve.bn_stats(stats[:, o + t, :], X[:, one_tile(tile + t), :].rearrange("p a d -> p (a d)"))
            link(ins)
            dve.memset(gate[:, :], 0.0)
            for t in range(n):
                ins = dve.bn_aggr(mv[:, o + t, :], stats[:, o + t, :])
            return ins

        def norm_rstd(pool, link, n, o=0):
            link(pool.tensor_tensor(veps[:, o:o + n], mv[:, o:o + n, 1], eps[:, 0:n], ALU.add))
            return pool.tensor_tensor(rstd[:, o:o + n], veps[:, o:o + n], minus_half[:, 0:n], ALU.pow)

        def norm_apply(dve, X, tile, n, dst, o=0):
            for t in range(n):
                ins = dve.tensor_scalar(dst[:, t, 0:D], X[:, one_tile(tile + t), :].rearrange("p a d -> p (a d)"),
                                        mv[:, o + t, 0:1], rstd[:, o + t:o + t + 1], ALU.subtract, ALU.mult)
            return ins

        f = {n: sem("f_" + n) for n in (
            "stats", "rstd", "normed", "xt_mm", "xt_ev", "h_mm", "gelu", "logit_mm", "shifted", "logit_exp",
            "alpha", "alt_mm", "alt_ev", "si_mm", "si", "sit_mm", "sit", "gi_mm", "gates", "gates_tanh", "n_in",
            "n_tanh", "new", "qkv_mm", "q", "kv", "score_mm", "score", "score_exp", "prob", "pt_mm", "pt", "y_mm",
            "y", "yt_mm", "yt", "so_mm", "so", "out_mm", "added", "ystats", "yrstd")}

        def early_norm(dve, link, kind, rep):
            k = rep * CHUNKS + 1
            if kind == "ffn_stats":
                norm_stats(dve, link, X, 0, CT, CT).then_inc(f["stats"], 1)
            else:
                dve.wait_ge(f["rstd"], k)
                norm_apply(dve, X, 0, CT, f_xs[0], CT).then_inc(f["normed"], 1)

        def early_rstd(pool, link, rep):
            pool.wait_ge(f["stats"], rep * CHUNKS + 1)
            norm_rstd(pool, link, CT, CT).then_inc(f["rstd"], 1)

        a_filled = sem("a_filled")
        a_stats, a_rstd, a_normed = sem("a_stats"), sem("a_rstd"), sem("a_normed")
        a_xh, a_xl = sem("a_xh"), sem("a_xl")
        a_hi, a_lo, a_values, a_maxrow = sem("a_hi"), sem("a_lo"), sem("a_values"), sem("a_maxrow")
        a_max_mm, a_maxed = sem("a_max_mm"), sem("a_maxed")
        a_exp_mm, a_exped, a_masked = sem("a_exp_mm"), sem("a_exped"), sem("a_masked")
        a_pv, a_normal, a_turned, a_added = sem("a_pv"), sem("a_normal"), sem("a_turned"), sem("a_added")

        def a_read(step, b):
            kind, g, j = step
            u = GA * b + g
            return {"qk": (a_lo, 2 * (u + 1) + j + 1), "v": (a_values, u + 2), "maxrow": (a_maxrow, u + 2),
                    "turn": (a_turned, u), "project": (a_added, b), "xt": (a_xl, b + 2)}[kind]

        def bank3(g, j):
            return (3 * g + j) % 2

        a_even = sem("a_even")

        def evens(u, exps):
            return 2 * u + exps + 1

        def a_tensor(pe):
            def do(step, b, fill):
                kind, g, j = step
                u = GA * b + g
                me, nx = g % 2, (g + 1) % 2
                if fill:
                    dst = R[fill.bank]
                    if fill.former:
                        wait(pe, *a_read(*fill.former))
                if kind == "xt":
                    pe.wait_ge(a_normed, b + 2)
                    for t in range(QT):
                        ins = pe.transpose(dst[:, t * 128:(t + 1) * 128], xn[:, t, :], ident[:, :])
                    ins.then_inc(a_filled, 1)
                elif kind == "qk":
                    pair = 2 * ((g + 1) % GA) + j
                    if g == GA - 1 and j == 0:
                        pe.wait_ge(a_xl, b + 2)
                    for z in range(2):
                        ins = mm3(pe, dst[:, z * SEQ:(z + 1) * SEQ], a_wqk_h[:, pair, z, :], a_wqk_l[:, pair, z, :],
                                  xh[:, :], xl[:, :], z == 0, z == 1)
                    ins.then_inc(a_filled, 1)
                elif kind == "v":
                    c = ((g + 1) % GA) * 4 * EA
                    for t in range(QT):
                        tok = slice(t * 128, t * 128 + 128)
                        ins = mm3(pe, dst[:, t * 256:(t + 1) * 256], xh[:, tok], xl[:, tok],
                                  a_wv_h[:, c:c + 256], a_wv_l[:, c:c + 256], t == 0, t == 1)
                    ins.then_inc(a_filled, 1)
                elif kind == "max":
                    m = 3 * (u + 1) + j
                    wait(pe, a_maxed, m - 1)
                    if j == 0:
                        pe.wait_ge(a_hi, 2 * (u + 1) + 2)
                    dst = M[bank3(g + 1, j)]
                    if j == 0:
                        for i, h in enumerate((0, 2, 1, 3)):
                            p = slice(64 * (h % 2), 64 * (h % 2) + 64)
                            if i == 2:
                                ins.then_inc(a_even, 1)
                                pe.matmul(dst[:, :], identb[:, :], w["mask_q"][:, :, :], start=False, stop=False,
                                          skip_group_check=True)
                                pe.wait_ge(a_even, evens(u + 1, 0))
                            ins = pe.matmul(dst[:, h * 128:(h + 1) * 128], a_qk_h[p, nx, h // 2, 0, 0:128],
                                            a_qk_h[p, nx, h // 2, 1, 0:128], start=i == 0, stop=i == 3,
                                            skip_group_check=True)
                    else:
                        p = slice(64 * (j - 1), 64 * (j - 1) + 64)
                        for pair in range(2):
                            pe.matmul(dst[:, pair * 256:(pair + 1) * 256], a_qk_h[p, nx, pair, 0, 128:256],
                                      a_qk_h[p, nx, pair, 1, :], start=pair == 0, stop=False, skip_group_check=True)
                        ins = pe.matmul(dst[:, :].rearrange("p (h k) -> p h k", h=2)[:, :, 128:256], identb[:, :],
                                        w["mask_q"][:, 0:2, :], start=False, stop=True, skip_group_check=True)
                    ins.then_inc(a_max_mm, 1)
                elif kind == "maxrow":
                    pe.wait_ge(a_maxed, 3 * (u + 1) + 3)
                    for t in range(QT):
                        ins = pe.transpose(RB16[fill.bank][0:4, t * 128:(t + 1) * 128], a_nm[:, nx, t, :],
                                           identb[:, :])
                    ins.then_inc(a_filled, 1)
                elif kind == "exps":
                    n = 3 * u + j
                    wait(pe, a_exped, n - 1)
                    if j == 0:
                        pe.wait_ge(a_lo, 2 * u + 2)
                    dst = T[bank3(g, j)]
                    heads, wd, q0, k0 = ((j, j + 2), 256, 0, 0) if j < 2 else ((0, 2, 1, 3), 128, 128, 128)
                    for i, h in enumerate(heads):
                        p, keys, qs = slice(64 * (h % 2), 64 * (h % 2) + 64), slice(k0, k0 + 128), slice(q0, 256)
                        if i == 2:
                            ins.then_inc(a_even, 1)
                            pe.wait_ge(a_even, evens(u, 1))
                        ins = mm3(pe, dst[:, i * wd:(i + 1) * wd],
                            a_qk_h[p, me, h // 2, 1, keys], a_qk_l[p, me, h // 2, 1, keys],
                            a_qk_h[p, me, h // 2, 0, qs], a_qk_l[p, me, h // 2, 0, qs], i == 0, False)
                    if j == 0:
                        pe.wait_ge(a_maxrow, u + 1)
                    for i, h in enumerate(heads):
                        ins = pe.matmul(dst[:, i * wd:(i + 1) * wd], w["onehot"][:, h, :], a_nmt[:, me, q0:256],
                                        start=False, stop=i == len(heads) - 1, skip_group_check=True)
                    ins.then_inc(a_exp_mm, 1)
                elif kind == "pv":
                    q = j
                    if q == 0:
                        pe.wait_ge(a_values, u + 1)
                        wait(pe, a_normal, u)
                    pe.wait_ge(a_masked, 3 * u + 2 + q)
                    for h in range(4):
                        for k in range(q + 1):
                            c = (h // 2) * 256 + q * 128 if k == 0 else (0, 2, 1, 3)[h] * 128
                            ins = pe.matmul(O[q][:, h * W:(h + 1) * W],
                                            a_p[:, me, h % 2 if k == 0 else 2, c:c + 128], a_v[:, me, k, h, :],
                                            start=h == 0 and k == 0, stop=h == 3 and k == q, skip_group_check=True)
                    ins.then_inc(a_pv, 1)
                elif kind == "turn":
                    if isinstance(b, int) and b == 0 and g == GA - 1:
                        pe.wait_ge(w_loaded, 16 * 2)
                    pe.wait_ge(a_normal, u)
                    for pair in range(2):
                        for t in range(QT):
                            c = (2 * pair + t) * 128
                            ins = pe.transpose(dst[:, c:c + 128], a_o[:, nx, t, 2 * pair:2 * pair + 2, :]
                                               .rearrange("p h e -> p (h e)"), ident[:, :])
                    ins.then_inc(a_filled, 1)
                elif kind == "project":
                    pe.wait_ge(a_turned, GA * b)
                    for t in range(QT):
                        for c in range(8):
                            ins = pe.matmul(dst[:, t * 128:(t + 1) * 128], a_ot[:, c, t * 128:(t + 1) * 128],
                                            w["a_wo"][:, c, :], start=c == 0, stop=c == 7)
                    ins.then_inc(a_filled, 1)
            run_plan(pe, A_PLAN, do)

        def a_scalar(act):
            def do(step, b, fill):
                kind, g, j = step
                u = GA * b + g
                me, nx = g % 2, (g + 1) % 2
                if kind in ("xt", "qk", "v", "turn"):
                    act.wait_ge(a_filled, fill.count)
                    src = R[fill.bank]
                if kind == "xt":
                    act.activation(xh[:, :], src[:, 0:SEQ], ACT.Copy).then_inc(a_xh, 1)
                elif kind == "qk":
                    act.activation(a_qk_h[:, nx, j, :, :].rearrange("p z t -> p (z t)"), src[:, :],
                                   ACT.Copy).then_inc(a_hi, 1)
                elif kind == "v":
                    act.activation(a_v[:, nx, :, :, 0:EA], src[:, :].rearrange("p (t h e) -> p t h e", t=QT, h=4),
                                   ACT.Copy, scale=1.0 / V_UP).then_inc(a_values, 1)
                elif kind == "exps":
                    act.wait_ge(a_exp_mm, 3 * u + j + 1)
                    act.activation(a_p[:, me, j, :], T[bank3(g, j)][:, :], ACT.Exp,
                                   scale=EA ** -0.5).then_inc(a_exped, 1)
                elif kind == "turn":
                    c = 2 * ((g - 1) % GA)
                    act.activation(a_ot[:, c:c + 2, :], src[:, :].rearrange("p (c t) -> p c t", c=2),
                                   ACT.Copy).then_inc(a_turned, 1)
            run_plan(act, A_PLAN, do)

        def a_vector(dve, chain):
            link = chain.link

            def do(step, b, fill):
                kind, g, j = step
                u = GA * b + g
                me, nx = g % 2, (g + 1) % 2
                if kind in ("ffn_stats", "ffn_apply"):
                    early_norm(dve, link, kind, 0)
                elif kind == "norm":
                    if isinstance(b, int) and b == 0:
                        dve.wait_ge(x_late, 16)
                    norm_stats(dve, link, X, (b + 1) * QT, QT).then_inc(a_stats, 1)
                elif kind == "apply":
                    dve.wait_ge(a_rstd, b + 2)
                    norm_apply(dve, X, (b + 1) * QT, QT, xn).then_inc(a_normed, 1)
                elif kind == "xt":
                    dve.wait_ge(a_xh, b + 2)
                    dve.tensor_tensor(xl[:, :], R[fill.bank][:, 0:SEQ], xh[:, :], ALU.subtract).then_inc(a_xl, 1)
                elif kind == "qk":
                    dve.wait_ge(a_hi, 2 * (u + 1) + j + 1)
                    dve.tensor_tensor(a_qk_l[:, nx, j, :, :].rearrange("p z t -> p (z t)"), R[fill.bank][:, :],
                                      a_qk_h[:, nx, j, :, :].rearrange("p z t -> p (z t)"),
                                      ALU.subtract).then_inc(a_lo, 1)
                elif kind == "max":
                    dve.wait_ge(a_max_mm, 3 * (u + 1) + j + 1)
                    dst = a_nm[:, nx, 0, :] if j == 0 else a_nm[:, nx, 1, j - 1:4:2]
                    dve.tensor_reduce(dst, M[bank3(g + 1, j)][:, :].rearrange("p (h k) -> p h k", h=4 if j == 0 else 2),
                                      X_AXIS, ALU.max, negate=True).then_inc(a_maxed, 1)
                elif kind == "maxrow":
                    dve.wait_ge(a_filled, fill.count)
                    dve.tensor_copy(a_nmt[:, nx, :], RB16[fill.bank][0:4, 0:SEQ]).then_inc(a_maxrow, 1)
                elif kind == "mask":
                    dve.wait_ge(a_exped, 3 * u + j + 1)
                    p = a_p[:, me, j, :].rearrange("p (h q) -> p h q", h=2 if j < 2 else 4)[:, :, 0:128]
                    dve.tensor_tensor(p, p, w["limit_k"][:, 0:2 if j < 2 else 4, :], ALU.min).then_inc(a_masked, 1)
                elif kind == "normal":
                    dve.wait_ge(a_pv, 2 * u + 2)
                    for q in range(QT):
                        o = O[q][:, 0:4 * W].rearrange("p (h e) -> p h e", h=4)
                        ins = dve.reciprocal(a_rs[:, q, :], o[:, :, EA:EA + 1].rearrange("p h a -> p (h a)"))
                    link(ins)
                    for q in range(QT):
                        o = O[q][:, 0:4 * W].rearrange("p (h e) -> p h e", h=4)
                        ins = dve.tensor_tensor(a_o[:, me, q, :, :], o[:, :, 0:EA],
                                                a_rs[:, q, :].unsqueeze(2).to_broadcast([128, 4, EA]), ALU.mult)
                    ins.then_inc(a_normal, 1)
                elif kind == "project":
                    dve.wait_ge(a_filled, fill.count)
                    xb = X[:, bass.ds((b - 1) * QT, QT), :]
                    dve.tensor_tensor(xb, R[fill.bank][:, 0:SEQ].rearrange("p (t d) -> p t d", t=QT), xb,
                                      ALU.add).then_inc(a_added, 1)
            run_plan(dve, A_PLAN, do, chain, 1 + GA)
            dve.wait_ge(a_added, NB)

        def a_gpsimd(pool, chain):
            def do(step, b, fill):
                if step[0] == "ffn_stats":
                    early_rstd(pool, chain.link, 0)
                elif step[0] == "norm":
                    pool.wait_ge(a_stats, b + 2)
                    norm_rstd(pool, chain.link, QT).then_inc(a_rstd, 1)
            run_plan(pool, A_PLAN, do, chain, 1)

        b_filled = sem("b_filled")
        b_stats, b_rstd, b_normed = sem("b_stats"), sem("b_rstd"), sem("b_normed")
        b_xh, b_xl, b_hi, b_lo, b_values = sem("b_xh"), sem("b_xl"), sem("b_hi"), sem("b_lo"), sem("b_values")
        b_rolled, b_multiplied, b_dotted = sem("b_rolled"), sem("b_multiplied"), sem("b_dotted")
        b_shifted, b_exped, b_weighed, b_normal = sem("b_shifted"), sem("b_exped"), sem("b_weighed"), sem("b_normal")
        b_raised, b_flipped = sem("b_raised"), sem("b_flipped")
        b_gathered, b_expanded, b_added = sem("b_gathered"), sem("b_expanded"), sem("b_added")

        def rolled_values(par, t, h0, n):
            v = b_v[:, par, t, h0:h0 + 1, 0:1]
            return bass.AP(v.tensor, v.offset, [list(v.ap[0]), [EB, n], [1, EB], [EB, H]])

        def rolled_exps(par, t, h0, n):
            x = b_e[:, par, t, 0:1, h0:h0 + 1]
            return bass.AP(x.tensor, x.offset, [list(x.ap[0]), [1, n], [0, EB], [H, H]])

        def b_read(step, i):
            kind, par, j = step
            b = 2 * i + par
            return {"qk": (b_lo, b + 3), "v": (b_values, b + 2), "project": (b_added, b - 1), "xt": (b_xl, b + 3)}[kind]

        def b_tensor(pe):
            bank = [None]

            def do(step, i, fill):
                kind, par, j = step
                b = 2 * i + par
                nx = 1 - par
                if fill:
                    dst = R[fill.bank]
                    if fill.former:
                        wait(pe, *b_read(*fill.former))
                if kind == "xt":
                    pe.wait_ge(b_normed, b + 3)
                    for t in range(QT):
                        ins = pe.transpose(dst[:, t * 128:(t + 1) * 128], xn[:, t, :], ident[:, :])
                    ins.then_inc(b_filled, 1)
                elif kind == "qk":
                    pe.wait_ge(b_xl, b + 3)
                    for z in range(2):
                        ins = mm3(pe, dst[:, z * SEQ:(z + 1) * SEQ], b_w_h[:, z, :], b_w_l[:, z, :],
                                  xh[:, :], xl[:, :], z == 0, z == 1)
                    ins.then_inc(b_filled, 1)
                elif kind == "v":
                    for t in range(QT):
                        tok = slice(t * 128, t * 128 + 128)
                        ins = mm3(pe, dst[:, t * 128:(t + 1) * 128], xh[:, tok], xl[:, tok],
                                  b_w_h[:, 2, :], b_w_l[:, 2, :], t == 0, t == 1)
                    ins.then_inc(b_filled, 1)
                elif kind == "roll":
                    m = ROLLS * (b + 1) + j
                    if j == 0:
                        pe.wait_ge(b_lo, b + 2)
                    wait(pe, b_multiplied, m - 1)
                    for e in range(2):
                        pe.matmul(T[j % 2][:, e * SEQ:(e + 1) * SEQ], w["roll"][:, 2 * j + e, :], b_kh[:, nx, :],
                                  start=e == 0, stop=False, skip_group_check=True)
                        ins = pe.matmul(T[j % 2][:, e * SEQ:(e + 1) * SEQ], w["roll"][:, 2 * j + e, :], b_kl[:, nx, :],
                                        start=False, stop=e == 1, skip_group_check=True)
                    ins.then_inc(b_rolled, 1)
                elif kind == "dots":
                    pe.wait_ge(b_multiplied, ROLLS * (b + 1) + 4 * j + 4)
                    wait(pe, b_raised, 2 * b + j + 1)
                    for n in range(4):
                        ins = pe.matmul(M[j][32 * n:32 * n + 32, :], w["heads"][:, :],
                                        b_prod[:, 4 * j + n, :, :].rearrange("p e t -> p (e t)"), start=True, stop=True)
                    ins.then_inc(b_dotted, 1)
                elif kind == "flip":
                    pe.wait_ge(b_raised, 2 * (b + 1) + j + 1)
                    if j == 0:
                        wait(pe, b_shifted, b)
                    for t in range(QT):
                        for e in range(2):
                            ins = pe.matmul(O[nx][:, t * 256 + 128 * j:t * 256 + 128 * j + 128]
                                            .rearrange("p (n e h) -> p n e h", n=4, e=2)[:, :, e, :],
                                            b_st[:, j, e * SEQ + t * 128:e * SEQ + t * 128 + 128],
                                            ident[:, :].rearrange("p (n h) -> p n h", n=4)[:, :, 0:H],
                                            start=True, stop=True)
                    ins.then_inc(b_flipped, 1)
                elif kind in ("project", "projects"):
                    if kind == "project":
                        pe.wait_ge(b_expanded, b - 1)
                        bank[0] = dst
                    t, half = divmod(j, 2)
                    out_t = bank[0][:, t * 128:(t + 1) * 128]
                    for e in range(half * EB // 2, (half + 1) * EB // 2):
                        pe.matmul(out_t, b_ox[:, par, t, e, :, :].rearrange("p h r -> p (h r)"), w["b_wo"][:, e, :],
                                  start=e == 0, stop=False)
                    if half:
                        ins = pe.matmul(out_t, ones[0:1, :], w["b_bo"][:, :], start=False, stop=True)
                    if j == 3:
                        ins.then_inc(b_filled, 1)
            run_plan(pe, B_PLAN, do)

        def b_scalar(act):
            def do(step, i, fill):
                kind, par, j = step
                b = 2 * i + par
                if kind in ("xt", "qk", "v"):
                    act.wait_ge(b_filled, fill.count)
                    src = R[fill.bank]
                if kind == "xt":
                    act.activation(xh[:, :], src[:, 0:SEQ], ACT.Copy).then_inc(b_xh, 1)
                elif kind == "qk":
                    act.activation(b_qt[:, par, :], src[:, 0:SEQ], ACT.Copy)
                    act.activation(b_kh[:, par, :], src[:, SEQ:2 * SEQ], ACT.Copy).then_inc(b_hi, 1)
                elif kind == "v":
                    wait(act, b_weighed, 3 * b)
                    for n in range(2):
                        ins = act.activation(b_v[:, 1 - par, :, n * H:(n + 1) * H, :].rearrange("p t h e -> p t (h e)"),
                                             src[:, 0:SEQ].rearrange("p (t c) -> p t c", t=QT), ACT.Copy)
                    ins.then_inc(b_values, 1)
                elif kind == "dots":
                    act.wait_ge(b_dotted, 2 * (b + 1) + j + 1)
                    act.activation(b_st[:, j, :], M[j][:, :], ACT.Copy).then_inc(b_raised, 1)
                elif kind == "soft":
                    act.wait_ge(b_shifted, b + 1)
                    act.activation(b_e[:, par, :, :, :], b_e[:, par, :, :, :], ACT.Exp, scale=EB ** -0.5).then_inc(b_exped, 1)
                elif kind == "expand":
                    act.wait_ge(b_normal, b)
                    wait(act, b_added, b - 2)
                    for r in range(TB):
                        for t in range(QT):
                            ins = act.activation(b_ox[:, 1 - par, t, :, :, r], b_o[:, t, :, :].rearrange("p h e -> p e h"),
                                                 ACT.Copy, scale=w["rowmask"][:, r:r + 1])
                    ins.then_inc(b_expanded, 1)
            run_plan(act, B_PLAN, do)

        def b_vector(dve, chain):
            link, bank = chain.link, [None]

            def do(step, i, fill):
                kind, par, j = step
                b = 2 * i + par
                if kind in ("ffn_stats", "ffn_apply"):
                    early_norm(dve, link, kind, 1)
                elif kind == "norm":
                    norm_stats(dve, link, X, (b + 2) * QT, QT).then_inc(b_stats, 1)
                elif kind == "apply":
                    dve.wait_ge(b_rstd, b + 3)
                    norm_apply(dve, X, (b + 2) * QT, QT, xn).then_inc(b_normed, 1)
                elif kind == "xt":
                    dve.wait_ge(b_xh, b + 3)
                    dve.tensor_tensor(xl[:, :], R[fill.bank][:, 0:SEQ], xh[:, :], ALU.subtract).then_inc(b_xl, 1)
                elif kind == "qk":
                    dve.wait_ge(b_hi, b + 3)
                    dve.tensor_tensor(b_kl[:, par, :], R[fill.bank][:, SEQ:2 * SEQ], b_kh[:, par, :],
                                      ALU.subtract).then_inc(b_lo, 1)
                elif kind == "roll":
                    dve.wait_ge(b_rolled, ROLLS * (b + 1) + j + 1)
                    if j % 4 == 0:
                        wait(dve, b_dotted, 2 * b + j // 4 + 1)
                    dve.tensor_tensor(b_prod[:, j, :, :], T[j % 2][:, :].rearrange("p (e t) -> p e t", e=2),
                                      b_qt[:, 1 - par, :].unsqueeze(1).to_broadcast([128, 2, SEQ]),
                                      ALU.mult).then_inc(b_multiplied, 1)
                elif kind == "soft":
                    dve.wait_ge(b_flipped, 2 * (b + 1))
                    sc = O[par][:, :].rearrange("p (t s h) -> p t s h", t=QT, s=H)
                    link(dve.tensor_reduce(b_m[:, :, :], sc.rearrange("p t s h -> p t h s"), X_AXIS, ALU.max))
                    dve.tensor_tensor(b_e[:, par, :, :, :], sc, b_m[:, :, :].unsqueeze(2).to_broadcast([128, QT, H, H]),
                                      ALU.subtract).then_inc(b_shifted, 1)
                elif kind == "sumexp":
                    dve.wait_ge(b_exped, b + 1)
                    link(dve.tensor_reduce(b_rs[:, par, :, :], b_e[:, par, :, :, :].rearrange("p t s h -> p t h s"),
                                           X_AXIS, ALU.add))
                    link(dve.reciprocal(b_rs[:, par, :, :].rearrange("p t h -> p (t h)"),
                                        b_rs[:, par, :, :].rearrange("p t h -> p (t h)")))
                elif kind == "weigh" and j == 0:
                    dve.wait_ge(b_values, b + 1)
                    link(dve.tensor_tensor(b_w8[:, 0, 0:HV, :, :], rolled_values(par, 0, 0, HV),
                                           rolled_exps(par, 0, 0, HV), ALU.mult))
                elif kind == "gather":
                    dve.wait_ge(b_weighed, 3 * b if j else 3 * b + 1)
                    ins = dve.tensor_reduce(b_s[:, par ^ j, j, :], b_w8[:, j, :, :, :].rearrange("p h e s -> p (h e) s"),
                                            X_AXIS, ALU.add)
                    if j == 1:
                        link(ins)
                    else:
                        ins.then_inc(b_gathered, 1)
                elif kind == "normal":
                    wait(dve, b_expanded, b - 1)
                    dve.tensor_tensor(b_o[:, :, :, :].rearrange("p t h e -> p (t h) e"),
                                      b_s[:, 1 - par, :, :].rearrange("p t (h e) -> p (t h) e", e=EB),
                                      b_rs[:, 1 - par, :, :].rearrange("p t h -> p (t h)").unsqueeze(2)
                                      .to_broadcast([128, QT * H, EB]), ALU.mult).then_inc(b_normal, 1)
                elif kind == "project":
                    bank[0] = R[fill.bank], fill.count
                elif kind == "add":
                    projected, count = bank[0]
                    dve.wait_ge(b_filled, count)
                    for t in range(QT):
                        for m in range(QT):
                            xb = X[64 * t:64 * t + 64, bass.ds((b - 2) * QT + m, 1), :].rearrange("p a d -> p (a d)")
                            ins = dve.tensor_tensor(xb, projected[64 * m:64 * m + 64, t * 128:(t + 1) * 128], xb,
                                                    ALU.add)
                    ins.then_inc(b_added, 1)
            run_plan(dve, B_PLAN, do, chain, 2 * 6)
            dve.wait_ge(b_added, NB)

        def b_gpsimd(pool, chain):
            def do(step, i, fill):
                kind, par, j = step
                b = 2 * i + par
                if kind == "ffn_stats":
                    early_rstd(pool, chain.link, 1)
                elif kind == "norm":
                    pool.wait_ge(b_stats, b + 3)
                    norm_rstd(pool, chain.link, QT).then_inc(b_rstd, 1)
                elif kind == "weigh":
                    t, heads = ((0, range(HV, H)), (1, range(0, H // 2)), (1, range(H // 2, H)))[j]
                    if j == 0:
                        pool.wait_ge(b_exped, b + 1)
                        pool.wait_ge(b_values, b + 1)
                        wait(pool, b_gathered, b)
                    elif j == 1:
                        wait(pool, b_normal, b)
                    for h in heads:
                        ins = pool.tensor_tensor(b_w8[:, t, h, :, :],
                                                 b_v[:, par, t, h:h + H, :].rearrange("p s e -> p e s"),
                                                 b_e[:, par, t, :, h].unsqueeze(1).to_broadcast([128, EB, H]), ALU.mult)
                    ins.then_inc(b_weighed, 1)
            run_plan(pool, B_PLAN, do, chain, 2)

        GROUPS = CT // 4

        def f_order(t):
            b, q = divmod(t, QT)
            return (b // 2) * 4 + q * 2 + b % 2

        def f_plan(do, rep):
            for kind, c in F_PLAN:
                do(kind, c, c + rep * CHUNKS + 1)

        def f_banks(c):
            return PS[4 * c:4 * c + 4], (PS[6:8], PS[4:6])[c]

        def f_tensor(pe, rep):
            def do(kind, c, k):
                v = chunk[c]
                B, L = f_banks(c)
                if kind == "hidden":
                    pe.wait_ge(f["normed"], k)
                    if c == 0:
                        pe.wait_ge((a_added, b_added)[rep], NB)
                    for n in range(GROUPS):
                        wait(pe, f["xt_ev"], (k - 1) * GROUPS + n - 1 if (c or n >= 2) else 0)
                        for t in range(4):
                            ins = pe.transpose(PS[n % 2][:, t * 128:(t + 1) * 128], v["xs"][:, 4 * n + t, 0:D], ident[:, :])
                        ins.then_inc(f["xt_mm"], 1)
                        if n >= 1:
                            router(pe, c, k, n - 1)
                    router(pe, c, k, GROUPS - 1)
                elif kind == "logits":
                    for t in range(CT):
                        if t % 4 == 0:
                            pe.wait_ge(f["gelu"], (k - 1) * GROUPS + t // 4 + 1)
                        o = f_order(t)
                        ins = pe.matmul(L[o // 8][:, (o % 8) * NS:(o % 8 + 1) * NS], f_h[:, t * 128:(t + 1) * 128],
                                        w2s[:, :], start=True, stop=True)
                    ins.then_inc(f["logit_mm"], 1)
                elif kind == "read":
                    pe.wait_ge(f["alpha"], k)
                    for p in range(PAIRS):
                        for par in range(2):
                            for q in range(QT):
                                ins = pe.matmul(B[p // 2][64 * par:64 * par + 64, (p % 2) * 129:(p % 2) * 129 + 129],
                                                v["al"][:, 4 * p + 2 * q + par, :], v["xs"][:, 4 * p + 2 * par + q, :],
                                                start=q == 0, stop=q == QT - 1)
                    ins.then_inc(f["si_mm"], 1)
                    for n in range(CT // 2):
                        ins = pe.transpose(B[2 + n // 4][:, (n % 4) * 128:(n % 4 + 1) * 128],
                                           v["al"][:, 2 * n:2 * n + 2, :].rearrange("p a s -> p (a s)"), ident[:, :])
                    ins.then_inc(f["alt_mm"], 1)
                elif kind == "inputs":
                    pe.wait_ge(f["si"], k)
                    for p in range(PAIRS):
                        ins = pe.transpose(B[0][:, p * 128:(p + 1) * 128], v["si"][:, p, :], ident[:, :])
                    ins.then_inc(f["sit_mm"], 1)
                    pe.wait_ge(f["sit"], k)
                    pe.wait_ge(f["alt_ev"], k)
                    for n in range(3):
                        ins = pe.matmul(B[1 + n][:, :], w["wih_t"][:, n * 128:(n + 1) * 128], v["sit"][:, :],
                                        start=True, stop=True)
                    ins.then_inc(f["gi_mm"], 1)
                elif kind == "qkv":
                    pe.wait_ge(f["new"], k)
                    pe.matmul(B[0][0:DQ, :], w["wq"][:, :], v["sn"][:, :], start=True, stop=True)
                    pe.matmul(B[1][0:DQ, :], w["wk"][:, :], v["sn"][:, :], start=True, stop=True)
                    for p in range(PAIRS):
                        pe.matmul(B[2][:, p * 128:(p + 1) * 128], v["sn"][:, p * 128:(p + 1) * 128], w["wv"][:, :],
                                  start=True, stop=False)
                        ins = pe.matmul(B[2][:, p * 128:(p + 1) * 128], ones[0:1, :], w["bv"][:, :],
                                        start=False, stop=True)
                    ins.then_inc(f["qkv_mm"], 1)
                elif kind == "scores":
                    pe.wait_ge(f["q"], k)
                    pe.wait_ge(f["kv"], k)
                    for p in range(PAIRS):
                        for par in range(2):
                            sl = slice(p * 128 + par * 64, p * 128 + par * 64 + 64)
                            ins = pe.matmul(B[3][64 * par:64 * par + 64, p * NS:(p + 1) * NS], v["q"][:, sl], v["k"][:, sl],
                                            start=True, stop=True)
                    ins.then_inc(f["score_mm"], 1)
                elif kind == "probs":
                    pe.wait_ge(f["prob"], k)
                    for p in range(PAIRS):
                        ins = pe.transpose(B[0][:, p * 128:(p + 1) * 128], v["p"][:, p, :], ident[:, :])
                    ins.then_inc(f["pt_mm"], 1)
                elif kind == "attend":
                    pe.wait_ge(f["pt"], k)
                    for p in range(PAIRS):
                        sl = slice(p * 128, (p + 1) * 128)
                        pe.matmul(B[1][:, sl], v["pt"][:, sl], v["v"][:, p, :], start=True, stop=False)
                        ins = pe.matmul(B[1][:, sl], v["sn"][:, sl], ident[:, :], start=False, stop=True)
                    ins.then_inc(f["y_mm"], 1)
                elif kind == "ynorm":
                    pe.wait_ge(f["y"], k)
                    for p in range(PAIRS):
                        ins = pe.transpose(B[2][:, p * 128:(p + 1) * 128], v["y"][:, p, :], ident[:, :])
                    ins.then_inc(f["yt_mm"], 1)
                elif kind == "values":
                    pe.wait_ge(f["yt"], k)
                    for p in range(PAIRS):
                        sl = slice(p * 128, (p + 1) * 128)
                        pe.matmul(B[3][:, sl], v["yt"][:, sl], wcomb[:, :], start=True, stop=False)
                        ins = pe.matmul(B[3][:, sl], ones[0:1, :], crow[:, :], start=False, stop=True)
                    ins.then_inc(f["so_mm"], 1)
                elif kind == "out":
                    pe.wait_ge(f["so"], k)
                    for n in range(4):
                        pp, par = divmod(n, 2)
                        for m in range(4):
                            p, q = 2 * pp + m // 2, m % 2
                            ins = pe.matmul(B[n][:, m * 128:(m + 1) * 128], v["alt"][64 * par:64 * par + 64, 2 * p + q, :],
                                            v["so"][64 * par:64 * par + 64, p, :], start=True, stop=True)
                        ins.then_inc(f["out_mm"], 1)

            def router(pe, c, k, n):
                pe.wait_ge(f["xt_ev"], (k - 1) * GROUPS + n + 1)
                wait(pe, f["gelu"], (k - 1) * GROUPS + n - 1 if (c or n >= 2) else 0)
                pe.matmul(PS[2 + n % 2][0:DH, :], w["w1a"][:, :], f_xt[:, n * 512:(n + 1) * 512],
                          start=True, stop=True).then_inc(f["h_mm"], 1)
            f_plan(do, rep)

        def f_scalar(act, rep):
            def do(kind, c, k):
                v = chunk[c]
                B = f_banks(c)[0]
                if kind == "hidden":
                    for n in range(GROUPS + 1):
                        if n < GROUPS:
                            act.wait_ge(f["xt_mm"], (k - 1) * GROUPS + n + 1)
                            act.activation(f_xt[:, n * 512:(n + 1) * 512], PS[n % 2][:, :], ACT.Copy).then_inc(f["xt_ev"], 1)
                        if n == 0 and c:
                            act.wait_ge(f["logit_mm"], k - 1)
                        if n >= 1:
                            act.wait_ge(f["h_mm"], (k - 1) * GROUPS + n)
                            act.activation(f_h[0:DH, (n - 1) * 512:n * 512], PS[2 + (n - 1) % 2][0:DH, :], ACT.Gelu,
                                           bias=c1[:, :]).then_inc(f["gelu"], 1)
                elif kind == "alpha":
                    act.wait_ge(f["shifted"], k)
                    act.activation(f_e[:, :, :], f_e[:, :, :], ACT.Exp).then_inc(f["logit_exp"], 1)
                elif kind == "read":
                    act.wait_ge(f["alt_mm"], k)
                    for n in range(2):
                        ins = act.activation(v["alt"][:, 4 * n:4 * n + 4, :].rearrange("p a s -> p (a s)"), B[2 + n][:, :],
                                             ACT.Copy)
                    ins.then_inc(f["alt_ev"], 1)
                elif kind == "inputs":
                    act.wait_ge(f["sit_mm"], k)
                    act.activation(v["sit"][:, :], B[0][:, :], ACT.Copy).then_inc(f["sit"], 1)
                elif kind == "gates":
                    act.wait_ge(f["gates"], k)
                    act.activation(v["r"][:, :], v["r"][:, :], ACT.Tanh, scale=0.5)
                    act.activation(v["zg"][:, :], v["zg"][:, :], ACT.Tanh, scale=0.5).then_inc(f["gates_tanh"], 1)
                elif kind == "candidate":
                    act.wait_ge(f["n_in"], k)
                    act.activation(v["n"][:, :], v["n"][:, :], ACT.Tanh, bias=w["bih"][:, 2:3]).then_inc(f["n_tanh"], 1)
                elif kind == "qkv":
                    act.wait_ge(f["qkv_mm"], k)
                    act.activation(v["q"][:, :], B[0][0:DQ, :], ACT.Identity, bias=w["bq"][:, :]).then_inc(f["q"], 1)
                elif kind == "scores":
                    act.wait_ge(f["score"], k)
                    act.activation(v["s"][:, :, :], v["s"][:, :, :], ACT.Exp, scale=DQ ** -0.5).then_inc(f["score_exp"], 1)
                elif kind == "probs":
                    act.wait_ge(f["pt_mm"], k)
                    act.activation(v["pt"][:, :], B[0][:, :], ACT.Copy).then_inc(f["pt"], 1)
                elif kind == "ynorm":
                    act.wait_ge(f["yt_mm"], k)
                    act.activation(v["yt"][:, :], B[2][:, :], ACT.Copy).then_inc(f["yt"], 1)
                elif kind == "values":
                    act.wait_ge(f["so_mm"], k)
                    act.activation(v["so"][:, :, :].rearrange("p a d -> p (a d)"), B[3][:, :], ACT.Copy).then_inc(f["so"], 1)
            f_plan(do, rep)

        def f_vector(dve, rep, chain):
            link = chain.link

            def pairs(ap):
                return ap.rearrange("p (a d) -> p a d", a=PAIRS)

            def slots(ap):
                return ap.rearrange("p (b s) -> p b s", s=NS)

            def do(kind, c, k):
                v = chunk[c]
                B, L = f_banks(c)
                if kind == "stats":
                    norm_stats(dve, link, X, c * CT, CT).then_inc(f["stats"], 1)
                elif kind == "apply":
                    dve.wait_ge(f["rstd"], k)
                    norm_apply(dve, X, c * CT, CT, v["xs"]).then_inc(f["normed"], 1)
                elif kind == "top":
                    dve.wait_ge(f["logit_mm"], k)
                    for t in range(CT):
                        ins = dve.max(f_v8[:, t, :], L[t // 8][:, (t % 8) * NS:(t % 8 + 1) * NS])
                    link(ins)
                    for n in range(2):
                        ins = dve.tensor_tensor(f_e[:, 8 * n:8 * n + 8, :], L[n][:, :].rearrange("p (t s) -> p t s", t=8),
                                                f_v8[:, 8 * n:8 * n + 8, 0:1].to_broadcast([128, 8, NS]), ALU.subtract)
                    ins.then_inc(f["shifted"], 1)
                    for t in range(CT):
                        ins = dve.match_replace(f_z[:, t, :], f_v8[:, t, :], L[t // 8][:, (t % 8) * NS:(t % 8 + 1) * NS],
                                                TAKEN)
                    link(ins)
                elif kind == "alpha":
                    dve.wait_ge(f["logit_exp"], k)
                    link(dve.scalar_tensor_tensor(v["al"][:, :, :], f_z[:, :, :], TAKEN, f_e[:, :, :],
                                                  ALU.is_equal, ALU.mult))
                    link(dve.tensor_reduce(f_sum[:, :], v["al"][:, :, :], X_AXIS, ALU.add))
                    link(dve.reciprocal(f_sum[:, :], f_sum[:, :]))
                    dve.tensor_tensor(v["al"][:, :, :], v["al"][:, :, :], f_sum[:, :].unsqueeze(2).to_broadcast([128, CT, NS]),
                                      ALU.mult).then_inc(f["alpha"], 1)
                elif kind == "slots":
                    dve.wait_ge(f["si_mm"], k)
                    for n in range(2):
                        si = B[n][:, 0:258].rearrange("p (a d) -> p a d", a=2)
                        ins = dve.tensor_scalar(v["den"][:, 2 * n:2 * n + 2], si[:, :, D:D + 1].rearrange("p a d -> p (a d)"),
                                                1e-8, None, ALU.add)
                    link(ins)
                    link(dve.reciprocal(v["den"][:, :], v["den"][:, :]))
                    for n in range(2):
                        si = B[n][:, 0:258].rearrange("p (a d) -> p a d", a=2)
                        ins = dve.tensor_tensor(v["si"][:, 2 * n:2 * n + 2, :], si[:, :, 0:D],
                                                v["den"][:, 2 * n:2 * n + 2].unsqueeze(2).to_broadcast([128, 2, D]), ALU.mult)
                    ins.then_inc(f["si"], 1)
                elif kind == "gates":
                    dve.wait_ge(f["gi_mm"], k)
                    for n, dst in ((0, v["r"]), (1, v["zg"])):
                        ins = dve.tensor_tensor(slots(dst[:, :]), slots(B[1 + n][:, :]),
                                                gate_h[:, n:n + 1, :].to_broadcast([128, CB, NS]), ALU.add)
                    ins.then_inc(f["gates"], 1)
                elif kind == "candidate":
                    dve.wait_ge(f["gates_tanh"], k)
                    link(dve.scalar_tensor_tensor(slots(v["t"][:, :]), slots(v["r"][:, :]), 1.0,
                                                  hn_half[:, :].unsqueeze(1).to_broadcast([128, CB, NS]),
                                                  ALU.add, ALU.mult))
                    dve.tensor_tensor(v["n"][:, :], B[3][:, :], v["t"][:, :], ALU.add).then_inc(f["n_in"], 1)
                elif kind == "new":
                    dve.wait_ge(f["n_tanh"], k)
                    link(dve.tensor_tensor(slots(v["t"][:, :]), w["slot_t"][:, :].unsqueeze(1).to_broadcast([128, CB, NS]),
                                           slots(v["n"][:, :]), ALU.subtract))
                    link(dve.scalar_tensor_tensor(v["zg"][:, :], v["zg"][:, :], 1.0, v["t"][:, :], ALU.add, ALU.mult))
                    dve.scalar_tensor_tensor(v["sn"][:, :], v["zg"][:, :], 0.5, v["n"][:, :],
                                             ALU.mult, ALU.add).then_inc(f["new"], 1)
                elif kind == "qkv":
                    dve.wait_ge(f["qkv_mm"], k)
                    dve.tensor_scalar(v["k"][:, :], B[1][0:DQ, :], w["bk"][:, :], None, ALU.add)
                    dve.tensor_copy(v["v"][:, :, :], pairs(B[2][:, :])).then_inc(f["kv"], 1)
                elif kind == "scores":
                    dve.wait_ge(f["score_mm"], k)
                    sc = pairs(B[3][:, 0:PAIRS * NS])
                    link(dve.tensor_reduce(v["m"][:, :], sc, X_AXIS, ALU.max))
                    dve.tensor_tensor(v["s"][:, :, :], sc, v["m"][:, :].unsqueeze(2).to_broadcast([128, PAIRS, NS]),
                                      ALU.subtract).then_inc(f["score"], 1)
                elif kind == "probs":
                    dve.wait_ge(f["score_exp"], k)
                    link(dve.tensor_reduce(v["rs"][:, :], v["s"][:, :, :], X_AXIS, ALU.add))
                    link(dve.reciprocal(v["rs"][:, :], v["rs"][:, :]))
                    for par in range(2):
                        p = slice(64 * par, 64 * par + 64)
                        ins = dve.tensor_tensor(v["p"][p, :, par * NS:(par + 1) * NS], v["s"][p, :, :],
                                                v["rs"][p, :].unsqueeze(2).to_broadcast([64, PAIRS, NS]), ALU.mult)
                    ins.then_inc(f["prob"], 1)
                elif kind == "attend":
                    dve.wait_ge(f["y_mm"], k)
                    y = pairs(B[1][:, :])
                    for p in range(PAIRS):
                        ins = dve.bn_stats(stats[:, c * CT + p, :], y[:, p, :])
                    link(ins)
                    for p in range(PAIRS):
                        ins = dve.bn_aggr(mv[:, c * CT + p, :], stats[:, c * CT + p, :])
                    ins.then_inc(f["ystats"], 1)
                elif kind == "ynorm":
                    dve.wait_ge(f["yrstd"], k)
                    for p in range(PAIRS):
                        n = c * CT + p
                        ins = dve.tensor_scalar(v["y"][:, p, :], pairs(B[1][:, :])[:, p, :], mv[:, n, 0:1], rstd[:, n:n + 1],
                                                ALU.subtract, ALU.mult)
                    ins.then_inc(f["y"], 1)
                elif kind == "out":
                    for n in range(4):
                        pp, par = divmod(n, 2)
                        dve.wait_ge(f["out_mm"], (k - 1) * 4 + n + 1)
                        t = c * CT + 8 * pp
                        xs = X[:, t:t + 8, :].rearrange("p (a r q) d -> p a r (q d)", a=2, r=2)[:, :, par, :]
                        dve.tensor_tensor(xs, B[n][:, :].rearrange("p (a e) -> p a e", a=2), xs,
                                          ALU.add).then_inc(f["added"], 1)
            f_plan(do, rep)
            dve.wait_ge(f["added"], (rep + 1) * CHUNKS * 4)

        def f_gpsimd(pool, rep, chain):
            def do(kind, c, k):
                if kind == "stats":
                    pool.wait_ge(f["stats"], k)
                    norm_rstd(pool, chain.link, CT).then_inc(f["rstd"], 1)
                elif kind == "attend":
                    pool.wait_ge(f["ystats"], k)
                    norm_rstd(pool, chain.link, PAIRS, c * CT).then_inc(f["yrstd"], 1)
            f_plan(do, rep)

        def set_tensor(pe):
            pe.wait_ge(w_loaded, 16 * 2)
            for n in range(3):
                pe.matmul(PS[4][:, n * NS:(n + 1) * NS], w["whh_t"][:, n * 128:(n + 1) * 128], w["slot_t"],
                          start=True, stop=True)
            pe.matmul(PS[5][:, 0:1], w["slot"], ones[0:NS, 0:1], start=True, stop=True)
            pe.matmul(PS[6][:, 0:1], w["wvp"], w["ln_b"], start=True, stop=True)
            pe.matmul(PS[7][:, 0:128], w["wvp_t"], w["wo"], start=True, stop=True).then_inc(set_mm, 1)
            pe.wait_ge(set_ev, 1)
            pe.matmul(PS[4][0:DH, 0:1], w["w1b"], slot_mean[:, :], start=True, stop=True)
            pe.matmul(PS[5][0:1, 0:128], cmid[:, :], w["wo"], start=True, stop=True).then_inc(set_mm, 1)
            pe.wait_ge(consts_set, 1)

        def set_vector(dve, link):
            dve.wait_ge(w_loaded, 16 * 2)
            link(dve.tensor_tensor(brz[:, :], w["bih"][:, 0:2], w["bhh"][:, 0:2], ALU.add))
            dve.wait_ge(set_mm, 1)
            for n in range(2):
                dve.tensor_scalar(gate_h[:, n, :], PS[4][:, n * NS:(n + 1) * NS], brz[:, n:n + 1], None, ALU.add)
            dve.tensor_scalar(hn_half[:, :], PS[4][:, 2 * NS:3 * NS], w["bhh"][:, 2:3], 0.5, ALU.add, ALU.mult)
            dve.tensor_scalar(slot_mean[:, :], PS[5][:, 0:1], 1.0 / NS, None, ALU.mult)
            dve.tensor_tensor(cmid[:, :], PS[6][:, 0:1], w["bvp"], ALU.add)
            dve.tensor_scalar(wcomb[:, :], PS[7][:, 0:128], w["ln_g"], None, ALU.mult).then_inc(set_ev, 1)
            link(dve.scalar_tensor_tensor(inv_tau[:, 0:1], w["tau"], -1.0, w["tau"], ALU.mult, ALU.max))
            link(dve.tensor_scalar(inv_tau[:, 0:1], inv_tau[:, 0:1], 0.1, None, ALU.add))
            link(dve.reciprocal(inv_tau[:, 1:2], inv_tau[:, 0:1]))
            dve.tensor_scalar(w2s[:, :], w["w2b"], inv_tau[:, 1:2], None, ALU.mult)
            link(dve.tensor_copy(b_w_h[:, :, :], w["b_wqkv"]))
            dve.tensor_tensor(b_w_l[:, :, :], w["b_wqkv"], b_w_h[:, :, :], ALU.subtract)
            dve.wait_ge(set_mm, 2)
            dve.tensor_tensor(c1[:, :], PS[4][0:DH, 0:1], w["b1"], ALU.add)
            dve.tensor_tensor(crow[:, :], PS[5][0:1, 0:128], w["bo"], ALU.add).then_inc(consts_set, 1)

        block = ctx.enter_context(nc.Block())

        @block.sync
        def _(sp):
            early = 2 * QT
            sp.dma_start(X[:, 0:early, :], x_in[:, 0:early, :]).then_inc(x_early, 16)
            for n in ("first", "masks", "limit"):
                sp.dma_start(packs[n][:, :], w_in[n]).then_inc(a_loaded, 16)
            sp.dma_start(X[:, early:NT, :], x_in[:, early:NT, :]).then_inc(x_late, 16)
            for n in ("rest", "rolls"):
                sp.dma_start(packs[n][:, :], w_in[n]).then_inc(w_loaded, 16)
            for c in range(CHUNKS):
                sp.wait_ge(f["added"], (CHUNKS + c + 1) * 4)
                sp.dma_start(out[:, c * CT:(c + 1) * CT, :], X[:, c * CT:(c + 1) * CT, :]).then_inc(stored, 16)
            sp.wait_ge(stored, 16 * CHUNKS)

        @block.gpsimd
        def _(pool):
            chain = Chain(pool, pool_chain)
            pool.memset(minus_half[:, :], -0.5)
            pool.memset(eps[:, :], EPS)
            pool.memset(ones[:, :], 1.0)
            pool.memset(a_v[:, :, :, :, EA:W], 1.0)
            for v in chunk:
                pool.memset(v["p"][:, :, :], 0.0)
                ins = pool.memset(v["xs"][:, :, D:D + 1], 1.0)
            ins.then_inc(pool_set, 1)
            pool.wait_ge(pool_set, 1)
            a_gpsimd(pool, chain)
            f_gpsimd(pool, 0, chain)
            b_gpsimd(pool, chain)
            f_gpsimd(pool, 1, chain)

        @block.scalar
        def _(act):
            act.wait_ge(dve_set, 1)
            a_scalar(act)
            act.wait_ge(consts_set, 1)
            f_scalar(act, 0)
            b_scalar(act)
            f_scalar(act, 1)

        @block.vector
        def _(dve):
            chain = Chain(dve, dve_chain)
            link = chain.link
            dve.memset(f_h[DH:DH + 1, :], 1.0)
            dve.wait_ge(a_loaded, 16 * 3)
            dve.wait_ge(x_early, 16)
            dve.wait_ge(pool_set, 1)
            dve.tensor_copy(a_wqk_h[:, :, :, :], w["a_wqk"][:, :, :, :])
            link(dve.tensor_scalar(a_wv_h[:, :], w["a_wv"][:, :], V_UP, None, ALU.mult))
            dve.tensor_tensor(a_wqk_l[:, :, :, :], w["a_wqk"][:, :, :, :], a_wqk_h[:, :, :, :], ALU.subtract)
            dve.scalar_tensor_tensor(a_wv_l[:, :], w["a_wv"][:, :], V_UP, a_wv_h[:, :],
                                     ALU.mult, ALU.subtract).then_inc(dve_set, 1)
            a_vector(dve, chain)
            set_vector(dve, link)
            f_vector(dve, 0, chain)
            b_vector(dve, chain)
            f_vector(dve, 1, chain)

        @block.tensor
        def _(pe):
            pe.wait_ge(pool_set, 1)
            pe.wait_ge(dve_set, 1)
            a_tensor(pe)
            set_tensor(pe)
            f_tensor(pe, 0)
            b_tensor(pe)
            f_tensor(pe, 1)


def token_of_partition():
    return np.array([16 * h + 8 * t + r for t in range(2) for h in range(8) for r in range(8)])


def constants():
    bf16 = mybir.dt.np(BF16)
    row = token_of_partition()
    later = np.where(row[None, :] > row[:, None], MASKED, 0.0)
    roll = np.zeros((128, H, 128), np.float16)
    for n in range(H):
        for h in range(H):
            for e in range(EB):
                roll[EB * ((h + n) % H) + e, n, EB * h + e] = 1.0
    heads = np.repeat(np.eye(H, 32, dtype=np.float32), EB, axis=0)
    rowmask = (row[:, None] // H == np.arange(TB)[None, :]).astype(np.float32)
    onehot = np.zeros((4, 4, 128), np.float32)
    for h in range(4):
        onehot[h, h, :] = 1.0
    return {
        "ident": np.eye(128, dtype=np.float32), "identb": np.eye(128).astype(bf16),
        "onehot": onehot.astype(bf16), "roll": roll, "heads": heads, "rowmask": rowmask,
        "mask_q": np.repeat(later[:, None, :], 4, 1).astype(bf16),
        "limit_k": np.repeat(np.where(later.T < 0, 0.0, LARGEST).astype(np.float32)[:, None, :], 4, 1),
    }


def kernel(**inputs):
    import concourse.bacc as bacc
    from concourse.bass_utils import run_bass_kernel_spmd

    def get(name):
        return np.asarray(inputs[name])

    def ffn(name):
        return get("L0_ffn_" + name)

    def column(v):
        return v.reshape(-1, 1)

    def flat_t(v):
        return v.reshape(H * EA, D).T

    wq, wk = (flat_t(get("L0_attn_a_w" + n)).reshape(D, 8, 1, 128) for n in "qk")
    arrays = constants()
    arrays.update({
        "a_wqk": np.concatenate([wq, wk], axis=2), "a_wv": flat_t(get("L0_attn_a_wv")),
        "a_wo": get("L0_attn_a_wo").T.reshape(8, 128, D).transpose(1, 0, 2),
        "b_wqkv": np.stack([get("L0_attn_b_W" + n).T for n in "qkv"], axis=1),
        "b_wo": get("L0_attn_b_Wo").T.reshape(H, EB, D)[token_of_partition() % H], "b_bo": get("L0_attn_b_bo").reshape(1, D),
        "slot": ffn("slot_init"), "slot_t": ffn("slot_init").T,
        "w1a": ffn("w1")[:D], "w1b": ffn("w1")[D:], "b1": column(ffn("b1")),
        "w2b": np.concatenate([ffn("w2"), ffn("b2").reshape(1, NS)]),
        "tau": np.broadcast_to(ffn("tau").reshape(1, 1), (NS + 1, 1)),
        "wih_t": ffn("Wih").T, "whh_t": ffn("Whh").T,
        "bih": ffn("bih").reshape(3, D).T, "bhh": ffn("bhh").reshape(3, D).T,
        "wq": ffn("wq"), "bq": column(ffn("bq")), "wk": ffn("wk"), "bk": column(ffn("bk")),
        "wv": ffn("wv"), "bv": ffn("bv").reshape(1, D),
        "ln_g": column(ffn("ln_g")), "ln_b": column(ffn("ln_b")),
        "wvp": ffn("wvp"), "wvp_t": ffn("wvp").T, "bvp": column(ffn("bvp")),
        "wo": ffn("wo"), "bo": ffn("bo").reshape(1, D),
    })
    place = token_of_partition()
    x = get("L0_attn_a_x")
    shape = x.shape
    x = x.reshape(NT, 128, D)[:, place, :].transpose(1, 0, 2)
    nc = bacc.Bacc("TRN2", target_bir_lowering=False, num_devices=1)
    feeds = {"x_dram": np.ascontiguousarray(x)}
    x_in = nc.dram_tensor("x_dram", list(x.shape), F32, kind="ExternalInput").ap()
    w_in = {}
    for pack, names in PACK_NAMES.items():
        flat = [arrays[name].reshape(arrays[name].shape[0], -1) for name in names]
        a = np.zeros((128, sum(v.shape[1] for v in flat)), flat[0].dtype)
        column = 0
        for v in flat:
            a[:v.shape[0], column:column + v.shape[1]] = v
            column += v.shape[1]
        feeds[pack + "_dram"] = a
        w_in[pack] = nc.dram_tensor(pack + "_dram", list(a.shape), mybir.dt.from_np(a.dtype), kind="ExternalInput").ap()
    out = nc.dram_tensor("out_dram", list(x.shape), F32, kind="ExternalOutput").ap()
    build(nc, x_in, w_in, {name: list(a.shape) for name, a in arrays.items()}, out)
    result = run_bass_kernel_spmd(nc, [feeds], core_ids=[0]).results[0]["out_dram"]
    y = np.empty((NT, 128, D), result.dtype)
    y[:, place, :] = result.transpose(1, 0, 2)
    return y.reshape(shape)
```
